# Optimizing a Trainium2 kernel written in Bass

```python
import numpy as np
import jax
import jax.numpy as jnp

def _softmax(x, axis=-1):
    return jax.nn.softmax(x, axis=axis)

def _gelu(x):
    return jax.nn.gelu(x, approximate=True)

def _silu(x):
    return jax.nn.silu(x)

def _sigmoid(x):
    return jax.nn.sigmoid(x)

def _layernorm(x, axis=-1, eps=1e-05):
    m = jnp.mean(x, axis=axis, keepdims=True)
    v = jnp.var(x, axis=axis, keepdims=True)
    return (x - m) / jnp.sqrt(v + eps)

def _scatter_add(tgt, idx, src, axis=0):
    return tgt.at[idx].add(src)

def _segment_sum(src, seg, n):
    return jax.ops.segment_sum(src, seg, n)
kernel_name = 'mk_perceiver_d2_seqx_r4_05fae7'

def setup_inputs(seed: int=0):
    np.random.seed(seed)
    _w = jnp.asarray

    def _rec_inputs():
        import jax
        import jax.numpy as jnp
        _rk = jax.random.key(seed)
        x = -0.0002928 + 1 * jax.random.normal(jax.random.fold_in(_rk, 1), (1, 128, 256), jnp.float32)
        _lenS = 128 - jax.random.randint(jax.random.fold_in(_rk, 7), (1,), 0, max(1, 128 // 4) + 1, jnp.int32)
        _lenS2 = 12544 - jax.random.randint(jax.random.fold_in(_rk, 8), (1,), 0, max(1, 12544 // 4) + 1, jnp.int32)
        _ctx_1024P = jax.random.normal(jax.random.fold_in(_rk, 11), (1, 16, 256), jnp.float32)
        _ctx_1024c = jax.random.dirichlet(jax.random.fold_in(_rk, 511), 0.3 * jnp.ones((16,), jnp.float32), (1, 12544))
        _ctx_1024t = jnp.einsum('bsk,bkd->bsd', _ctx_1024c, _ctx_1024P)
        _ctx_1024t = _ctx_1024t * jax.lax.rsqrt(jnp.mean(jnp.square(_ctx_1024t)) + 1e-12) * 0.953939
        ctx_1024 = 2.81802e-05 + 1.00001 * (_ctx_1024t + 0.3 * jax.random.normal(jax.random.fold_in(_rk, 611), (1, 12544, 256), jnp.float32))
        return (x, ctx_1024)
    x, ctx_1024 = _rec_inputs()

    def _L0_xattn_setup():
        import jax, jax.numpy as jnp
        import numpy as np
        D_MODEL = 256
        NUM_HEADS = 16
        STRIDE_LIST = [1, 2, 4, 8, 1, 2, 4, 8, 1, 2, 4, 8, 1, 2, 4, 8]
        HEAD_DIM = D_MODEL // NUM_HEADS
        key = jax.random.key(seed)
        ks = jax.random.split(key, 8)
        B, T, S = (4, 256, 1024)
        w_scale = 0.02
        return {'decoder_input': jax.random.normal(ks[0], (B, T, D_MODEL), jnp.float32), 'encoder_output': jax.random.normal(ks[1], (B, S, D_MODEL), jnp.float32), 'Wq': jax.random.normal(ks[2], (D_MODEL, D_MODEL), jnp.float32) * w_scale, 'bq': jnp.zeros((D_MODEL,), jnp.float32), 'Wk': jax.random.normal(ks[3], (D_MODEL, D_MODEL), jnp.float32) * w_scale, 'bk': jnp.zeros((D_MODEL,), jnp.float32), 'Wv': jax.random.normal(ks[4], (D_MODEL, D_MODEL), jnp.float32) * w_scale, 'bv': jnp.zeros((D_MODEL,), jnp.float32), 'Wo': jax.random.normal(ks[5], (D_MODEL, D_MODEL), jnp.float32) * w_scale, 'bo': jnp.zeros((D_MODEL,), jnp.float32)}
    _L0_xattn_all = _L0_xattn_setup()
    _L0_xattn_in = {k: v for k, v in _L0_xattn_all.items() if k in ('Wq', 'bq', 'Wk', 'bk', 'Wv', 'bv', 'Wo', 'bo')}
    del _L0_xattn_all

    def _L0_attn_setup():
        import jax, jax.numpy as jnp
        import numpy as np
        import math
        B, S, E = (2, 512, 256)
        H, DK, DV = (16, 64, 64)

        def _rope(q, k):
            D = q.shape[-1]
            theta = 10000.0 ** (jnp.arange(0, D, 2, dtype=jnp.float32) / D)
            pos = jnp.arange(q.shape[-2], dtype=jnp.float32)
            freqs = pos[:, None] * (1.0 / theta)[None, :]
            emb = jnp.concatenate([freqs, freqs], axis=-1)
            cos = jnp.cos(emb)[None, None]
            sin = jnp.sin(emb)[None, None]

            def rotate(x):
                x1 = x[..., ::2]
                x2 = x[..., 1::2]
                return jnp.stack([-x2, x1], axis=-1).reshape(x.shape)
            return (q * cos + rotate(q) * sin, k * cos + rotate(k) * sin)
        key = jax.random.key(seed)
        ks = jax.random.split(key, 9)
        sE = 1.0 / math.sqrt(E)
        sV = 1.0 / math.sqrt(H * DV)
        return {'x': jax.random.normal(ks[0], (B, S, E), dtype=jnp.float32), 'wq': jax.random.uniform(ks[1], (H * DK, E), jnp.float32, -sE, sE), 'bq': jax.random.uniform(ks[2], (H * DK,), jnp.float32, -sE, sE), 'wk': jax.random.uniform(ks[3], (H * DK, E), jnp.float32, -sE, sE), 'bk': jax.random.uniform(ks[4], (H * DK,), jnp.float32, -sE, sE), 'wv': jax.random.uniform(ks[5], (H * DV, E), jnp.float32, -sE, sE), 'bv': jax.random.uniform(ks[6], (H * DV,), jnp.float32, -sE, sE), 'wo': jax.random.uniform(ks[7], (E, H * DV), jnp.float32, -sV, sV), 'bo': jax.random.uniform(ks[8], (E,), jnp.float32, -sV, sV)}
    _L0_attn_all = _L0_attn_setup()
    _L0_attn_in = {k: v for k, v in _L0_attn_all.items() if k in ('wq', 'bq', 'wk', 'bk', 'wv', 'bv', 'wo', 'bo')}
    del _L0_attn_all

    def _L0_ffn_setup():
        import jax, jax.numpy as jnp
        import numpy as np
        E = 32
        H = 256
        I = 128
        G = 8
        TKG = 4
        TOPK = 8
        NSH = 2
        SCALE = 2.5
        key = jax.random.key(seed)
        ks = jax.random.split(key, 10)
        s = 0.02
        return {'hidden_states': jax.random.normal(ks[0], (2, 256, H), jnp.float32), 'gate_w': jax.random.normal(ks[1], (E, H), jnp.float32) * s, 'gate_bias': jax.random.normal(ks[2], (E,), jnp.float32) * s, 'w_gate': jax.random.normal(ks[3], (E, I, H), jnp.float32) * s, 'w_up': jax.random.normal(ks[4], (E, I, H), jnp.float32) * s, 'w_down': jax.random.normal(ks[5], (E, H, I), jnp.float32) * s, 'sh_gate': jax.random.normal(ks[6], (I * NSH, H), jnp.float32) * s, 'sh_up': jax.random.normal(ks[7], (I * NSH, H), jnp.float32) * s, 'sh_down': jax.random.normal(ks[8], (H, I * NSH), jnp.float32) * s}
    _L0_ffn_all = _L0_ffn_setup()
    _L0_ffn_in = {k: v for k, v in _L0_ffn_all.items() if k in ('gate_w', 'gate_bias', 'w_gate', 'w_up', 'w_down', 'sh_gate', 'sh_up', 'sh_down')}
    del _L0_ffn_all

    def _L1_xattn_setup():
        import jax, jax.numpy as jnp
        import numpy as np
        from jax import lax
        BIG = jnp.float32(1e+30)

        def _pairwise_euclidean(a, b):
            aa = jnp.sum(a * a, axis=-1)[:, None]
            bb = jnp.sum(b * b, axis=-1)[None, :]
            ab = a @ b.T
            return jnp.sqrt(jnp.maximum(aa + bb - 2.0 * ab, 0.0))

        def _dtw_cost(D):
            row0 = jnp.cumsum(D[0])

            def row_step(prev_row, d_row):
                first = d_row[0] + prev_row[0]

                def col_step(left, inp):
                    d_ij, up, diag = inp
                    r = d_ij + jnp.minimum(jnp.minimum(up, left), diag)
                    return (r, r)
                _, rest = lax.scan(col_step, first, (d_row[1:], prev_row[1:], prev_row[:-1]))
                row = jnp.concatenate([first[None], rest])
                return (row, row)
            _, rows = lax.scan(row_step, row0, D[1:])
            return jnp.concatenate([row0[None], rows], axis=0)

        def _backtrack(R, T1, T2):
            L = T1 + T2 - 1

            def step(carry, _):
                i, j, done = carry
                valid = jnp.logical_not(done)
                cd = jnp.where((i > 0) & (j > 0), R[jnp.maximum(i - 1, 0), jnp.maximum(j - 1, 0)], BIG)
                cu = jnp.where(i > 0, R[jnp.maximum(i - 1, 0), j], BIG)
                cl = jnp.where(j > 0, R[i, jnp.maximum(j - 1, 0)], BIG)
                choice = jnp.argmin(jnp.stack([cd, cu, cl]))
                ni = jnp.where(choice <= 1, i - 1, i)
                nj = jnp.where((choice == 0) | (choice == 2), j - 1, j)
                at_origin = (i == 0) & (j == 0)
                ni = jnp.where(at_origin, 0, ni)
                nj = jnp.where(at_origin, 0, nj)
                return ((ni, nj, done | at_origin), (i, j, valid))
            init = (jnp.int32(T1 - 1), jnp.int32(T2 - 1), jnp.bool_(False))
            _, (i_idx, j_idx, valid) = lax.scan(step, init, None, length=L)
            return (i_idx, j_idx, valid)

        def _align_one(small, large):
            T_small, d = small.shape
            T_large = large.shape[0]
            D = _pairwise_euclidean(small, large)
            R = _dtw_cost(D)
            i_idx, j_idx, valid = _backtrack(R, T_small, T_large)
            contrib = small[i_idx] * valid[:, None].astype(small.dtype)
            expanded = jnp.zeros((T_large, d), dtype=small.dtype).at[j_idx].add(contrib)
            return expanded
        key = jax.random.key(seed)
        k1, k2 = jax.random.split(key)
        teacher = jax.random.normal(k1, (16, 100, 256), dtype=jnp.float32)
        student = jax.random.normal(k2, (16, 150, 256), dtype=jnp.float32)
        return {'teacher_features': teacher, 'student_features': student}
    _L1_xattn_all = _L1_xattn_setup()
    _L1_xattn_in = {k: v for k, v in _L1_xattn_all.items() if k in ()}
    del _L1_xattn_all

    def _L1_attn_setup():
        import jax, jax.numpy as jnp
        import numpy as np
        B, L, D = (2, 512, 256)
        H, HD = (16, 64)
        LD = 64
        key = jax.random.key(seed)
        ks = jax.random.split(key, 6)
        s = lambda fan_in: 1.0 / np.sqrt(fan_in)
        x_bld = jax.random.normal(ks[0], (B, L, D), dtype=jnp.float32)
        Wq = jax.random.normal(ks[1], (D, H, HD), dtype=jnp.float32) * s(D)
        Wkv_down = jax.random.normal(ks[2], (D, LD), dtype=jnp.float32) * s(D)
        Wk_up = jax.random.normal(ks[3], (LD, H, HD), dtype=jnp.float32) * s(LD)
        Wv_up = jax.random.normal(ks[4], (LD, H, HD), dtype=jnp.float32) * s(LD)
        Wout = jax.random.normal(ks[5], (H, HD, D), dtype=jnp.float32) * s(H * HD)
        return {'x_bld': x_bld, 'Wq': Wq, 'Wkv_down': Wkv_down, 'Wk_up': Wk_up, 'Wv_up': Wv_up, 'Wout': Wout}
    _L1_attn_all = _L1_attn_setup()
    _L1_attn_in = {k: v for k, v in _L1_attn_all.items() if k in ('Wq', 'Wkv_down', 'Wk_up', 'Wv_up', 'Wout')}
    del _L1_attn_all

    def _L1_ffn_setup():
        import jax, jax.numpy as jnp
        import numpy as np
        B, T, D, E, H = (8, 512, 256, 8, 64)
        LN_EPS = 1e-05
        key = jax.random.key(seed)
        ks = jax.random.split(key, 4)
        return {'x': jax.random.normal(ks[0], (B, T, D), dtype=jnp.float32), 'Wg': jax.random.normal(ks[1], (E, D), dtype=jnp.float32) * 0.02, 'ln_scale': jnp.ones((E, D), dtype=jnp.float32), 'ln_bias': jnp.zeros((E, D), dtype=jnp.float32), 'W1': jax.random.normal(ks[2], (E, D, H), dtype=jnp.float32) * 0.02, 'b1': jnp.zeros((E, H), dtype=jnp.float32), 'W2': jax.random.normal(ks[3], (E, H, D), dtype=jnp.float32) * 0.02, 'b2': jnp.zeros((E, D), dtype=jnp.float32)}
    _L1_ffn_all = _L1_ffn_setup()
    _L1_ffn_in = {k: v for k, v in _L1_ffn_all.items() if k in ('Wg', 'ln_scale', 'ln_bias', 'W1', 'b1', 'W2', 'b2')}
    del _L1_ffn_all
    return {'x': x, 'ctx_1024': ctx_1024, 'L0_xattn_Wq': _L0_xattn_in['Wq'], 'L0_xattn_bq': _L0_xattn_in['bq'], 'L0_xattn_Wk': _L0_xattn_in['Wk'], 'L0_xattn_bk': _L0_xattn_in['bk'], 'L0_xattn_Wv': _L0_xattn_in['Wv'], 'L0_xattn_bv': _L0_xattn_in['bv'], 'L0_xattn_Wo': _L0_xattn_in['Wo'], 'L0_xattn_bo': _L0_xattn_in['bo'], 'L0_attn_wq': _L0_attn_in['wq'], 'L0_attn_bq': _L0_attn_in['bq'], 'L0_attn_wk': _L0_attn_in['wk'], 'L0_attn_bk': _L0_attn_in['bk'], 'L0_attn_wv': _L0_attn_in['wv'], 'L0_attn_bv': _L0_attn_in['bv'], 'L0_attn_wo': _L0_attn_in['wo'], 'L0_attn_bo': _L0_attn_in['bo'], 'L0_ffn_gate_w': _L0_ffn_in['gate_w'], 'L0_ffn_gate_bias': _L0_ffn_in['gate_bias'], 'L0_ffn_w_gate': _L0_ffn_in['w_gate'], 'L0_ffn_w_up': _L0_ffn_in['w_up'], 'L0_ffn_w_down': _L0_ffn_in['w_down'], 'L0_ffn_sh_gate': _L0_ffn_in['sh_gate'], 'L0_ffn_sh_up': _L0_ffn_in['sh_up'], 'L0_ffn_sh_down': _L0_ffn_in['sh_down'], 'L1_attn_Wq': _L1_attn_in['Wq'], 'L1_attn_Wkv_down': _L1_attn_in['Wkv_down'], 'L1_attn_Wk_up': _L1_attn_in['Wk_up'], 'L1_attn_Wv_up': _L1_attn_in['Wv_up'], 'L1_attn_Wout': _L1_attn_in['Wout'], 'L1_ffn_Wg': _L1_ffn_in['Wg'], 'L1_ffn_ln_scale': _L1_ffn_in['ln_scale'], 'L1_ffn_ln_bias': _L1_ffn_in['ln_bias'], 'L1_ffn_W1': _L1_ffn_in['W1'], 'L1_ffn_b1': _L1_ffn_in['b1'], 'L1_ffn_W2': _L1_ffn_in['W2'], 'L1_ffn_b2': _L1_ffn_in['b2']}

def reference(x, ctx_1024, L0_xattn_Wq, L0_xattn_bq, L0_xattn_Wk, L0_xattn_bk, L0_xattn_Wv, L0_xattn_bv, L0_xattn_Wo, L0_xattn_bo, L0_attn_wq, L0_attn_bq, L0_attn_wk, L0_attn_bk, L0_attn_wv, L0_attn_bv, L0_attn_wo, L0_attn_bo, L0_ffn_gate_w, L0_ffn_gate_bias, L0_ffn_w_gate, L0_ffn_w_up, L0_ffn_w_down, L0_ffn_sh_gate, L0_ffn_sh_up, L0_ffn_sh_down, L1_attn_Wq, L1_attn_Wkv_down, L1_attn_Wk_up, L1_attn_Wv_up, L1_attn_Wout, L1_ffn_Wg, L1_ffn_ln_scale, L1_ffn_ln_bias, L1_ffn_W1, L1_ffn_b1, L1_ffn_W2, L1_ffn_b2):
    import jax
    import jax.numpy as jnp

    def _L0_xattn_ref(decoder_input, encoder_output, Wq, bq, Wk, bk, Wv, bv, Wo, bo):
        import jax, jax.numpy as jnp
        import numpy as np
        D_MODEL = 256
        NUM_HEADS = 16
        STRIDE_LIST = [1, 2, 4, 8, 1, 2, 4, 8, 1, 2, 4, 8, 1, 2, 4, 8]
        HEAD_DIM = D_MODEL // NUM_HEADS
        B, T, _ = decoder_input.shape
        S = encoder_output.shape[1]
        Q = decoder_input @ Wq.T + bq
        K = encoder_output @ Wk.T + bk
        V = encoder_output @ Wv.T + bv
        Q = Q.reshape(B, T, NUM_HEADS, HEAD_DIM).transpose(0, 2, 1, 3)
        K = K.reshape(B, S, NUM_HEADS, HEAD_DIM).transpose(0, 2, 1, 3)
        V = V.reshape(B, S, NUM_HEADS, HEAD_DIM).transpose(0, 2, 1, 3)
        scale = 1.0 / HEAD_DIM ** 0.5
        head_outs = []
        for h in range(NUM_HEADS):
            s = STRIDE_LIST[h]
            K_h = K[:, h, ::s, :]
            V_h = V[:, h, ::s, :]
            scores = jnp.einsum('btd,bsd->bts', Q[:, h], K_h) * scale
            attn = jax.nn.softmax(scores, axis=-1)
            head_outs.append(jnp.einsum('bts,bsd->btd', attn, V_h))
        out = jnp.stack(head_outs, axis=2).reshape(B, T, D_MODEL)
        return out @ Wo.T + bo

    def _L0_attn_ref(x, wq, bq, wk, bk, wv, bv, wo, bo):
        import jax, jax.numpy as jnp
        import numpy as np
        import math
        B, S, E = (2, 512, 256)
        H, DK, DV = (16, 64, 64)

        def _rope(q, k):
            D = q.shape[-1]
            theta = 10000.0 ** (jnp.arange(0, D, 2, dtype=jnp.float32) / D)
            pos = jnp.arange(q.shape[-2], dtype=jnp.float32)
            freqs = pos[:, None] * (1.0 / theta)[None, :]
            emb = jnp.concatenate([freqs, freqs], axis=-1)
            cos = jnp.cos(emb)[None, None]
            sin = jnp.sin(emb)[None, None]

            def rotate(x):
                x1 = x[..., ::2]
                x2 = x[..., 1::2]
                return jnp.stack([-x2, x1], axis=-1).reshape(x.shape)
            return (q * cos + rotate(q) * sin, k * cos + rotate(k) * sin)
        Bx, Sx, Ex = x.shape
        q = (x @ wq.T + bq).reshape(Bx, Sx, H, DK).transpose(0, 2, 1, 3)
        k = (x @ wk.T + bk).reshape(Bx, Sx, H, DK).transpose(0, 2, 1, 3)
        v = (x @ wv.T + bv).reshape(Bx, Sx, H, DV).transpose(0, 2, 1, 3)
        q, k = _rope(q, k)
        scores = jnp.einsum('bhqd,bhkd->bhqk', q, k)
        causal = jnp.triu(jnp.ones((Sx, Sx), dtype=bool), k=1)
        scores = jnp.where(causal[None, None], -jnp.inf, scores)
        attn = jax.nn.softmax(scores / math.sqrt(DK), axis=-1)
        out = jnp.einsum('bhqk,bhkd->bhqd', attn, v)
        out = out.transpose(0, 2, 1, 3).reshape(Bx, Sx, H * DV)
        return out @ wo.T + bo

    def _L0_ffn_ref(hidden_states, gate_w, gate_bias, w_gate, w_up, w_down, sh_gate, sh_up, sh_down):
        import jax, jax.numpy as jnp
        import numpy as np
        E = 32
        H = 256
        I = 128
        G = 8
        TKG = 4
        TOPK = 8
        NSH = 2
        SCALE = 2.5
        B, S, Hd = hidden_states.shape
        h = hidden_states.reshape(-1, Hd)
        logits = h.astype(jnp.float32) @ gate_w.T
        scores = jax.nn.sigmoid(logits)
        sc = scores + gate_bias
        grp = sc.reshape(-1, G, E // G)
        group_scores = jax.lax.top_k(grp, 2)[0].sum(-1)
        gidx = jax.lax.top_k(group_scores, TKG)[1]
        gmask = jnp.sum(jax.nn.one_hot(gidx, G, dtype=sc.dtype), axis=1)
        smask = jnp.repeat(gmask, E // G, axis=1)
        masked = jnp.where(smask > 0, sc, jnp.zeros_like(sc))
        tki = jax.lax.top_k(masked, TOPK)[1]
        tkw = jnp.take_along_axis(scores, tki, axis=1)
        tkw = tkw / (tkw.sum(-1, keepdims=True) + 1e-20)
        tkw = tkw * SCALE
        combine = (jax.nn.one_hot(tki, E, dtype=tkw.dtype) * tkw[..., None]).sum(1)
        g = jax.nn.silu(jnp.einsum('th,eih->tei', h, w_gate))
        u = jnp.einsum('th,eih->tei', h, w_up)
        routed = jnp.einsum('tei,ehi->th', g * u * combine[:, :, None], w_down)
        sg = jax.nn.silu(h @ sh_gate.T)
        shared = sg * (h @ sh_up.T) @ sh_down.T
        return (routed + shared).reshape(B, S, Hd)

    def _L1_xattn_ref(teacher_features, student_features):
        import jax, jax.numpy as jnp
        import numpy as np
        from jax import lax
        BIG = jnp.float32(1e+30)

        def _pairwise_euclidean(a, b):
            aa = jnp.sum(a * a, axis=-1)[:, None]
            bb = jnp.sum(b * b, axis=-1)[None, :]
            ab = a @ b.T
            return jnp.sqrt(jnp.maximum(aa + bb - 2.0 * ab, 0.0))

        def _dtw_cost(D):
            row0 = jnp.cumsum(D[0])

            def row_step(prev_row, d_row):
                first = d_row[0] + prev_row[0]

                def col_step(left, inp):
                    d_ij, up, diag = inp
                    r = d_ij + jnp.minimum(jnp.minimum(up, left), diag)
                    return (r, r)
                _, rest = lax.scan(col_step, first, (d_row[1:], prev_row[1:], prev_row[:-1]))
                row = jnp.concatenate([first[None], rest])
                return (row, row)
            _, rows = lax.scan(row_step, row0, D[1:])
            return jnp.concatenate([row0[None], rows], axis=0)

        def _backtrack(R, T1, T2):
            L = T1 + T2 - 1

            def step(carry, _):
                i, j, done = carry
                valid = jnp.logical_not(done)
                cd = jnp.where((i > 0) & (j > 0), R[jnp.maximum(i - 1, 0), jnp.maximum(j - 1, 0)], BIG)
                cu = jnp.where(i > 0, R[jnp.maximum(i - 1, 0), j], BIG)
                cl = jnp.where(j > 0, R[i, jnp.maximum(j - 1, 0)], BIG)
                choice = jnp.argmin(jnp.stack([cd, cu, cl]))
                ni = jnp.where(choice <= 1, i - 1, i)
                nj = jnp.where((choice == 0) | (choice == 2), j - 1, j)
                at_origin = (i == 0) & (j == 0)
                ni = jnp.where(at_origin, 0, ni)
                nj = jnp.where(at_origin, 0, nj)
                return ((ni, nj, done | at_origin), (i, j, valid))
            init = (jnp.int32(T1 - 1), jnp.int32(T2 - 1), jnp.bool_(False))
            _, (i_idx, j_idx, valid) = lax.scan(step, init, None, length=L)
            return (i_idx, j_idx, valid)

        def _align_one(small, large):
            T_small, d = small.shape
            T_large = large.shape[0]
            D = _pairwise_euclidean(small, large)
            R = _dtw_cost(D)
            i_idx, j_idx, valid = _backtrack(R, T_small, T_large)
            contrib = small[i_idx] * valid[:, None].astype(small.dtype)
            expanded = jnp.zeros((T_large, d), dtype=small.dtype).at[j_idx].add(contrib)
            return expanded
        return jax.vmap(_align_one)(teacher_features, student_features)

    def _L1_attn_ref(x_bld, Wq, Wkv_down, Wk_up, Wv_up, Wout):
        import jax, jax.numpy as jnp
        import numpy as np
        B, L, D = (2, 512, 256)
        H, HD = (16, 64)
        LD = 64
        q_blhd = jnp.einsum('bld,dhk->blhk', x_bld, Wq)
        latent_bll = jnp.einsum('bld,dc->blc', x_bld, Wkv_down)
        k_blhd = jnp.einsum('blc,chk->blhk', latent_bll, Wk_up)
        v_blhd = jnp.einsum('blc,chk->blhk', latent_bll, Wv_up)
        attn = jnp.einsum('bqhd,bkhd->bhqk', q_blhd, k_blhd) / jnp.sqrt(jnp.asarray(HD, dtype=x_bld.dtype))
        l = x_bld.shape[1]
        mask = (jnp.arange(l)[None, :] <= jnp.arange(l)[:, None])[None, None]
        neg_inf = jnp.finfo(attn.dtype).min
        attn = jax.nn.softmax(jnp.where(mask, attn, neg_inf), axis=-1)
        y_blhd = jnp.einsum('bhqk,bkhd->bqhd', attn, v_blhd)
        return jnp.einsum('bqhd,hdo->bqo', y_blhd, Wout)

    def _L1_ffn_ref(x, Wg, ln_scale, ln_bias, W1, b1, W2, b2):
        import jax, jax.numpy as jnp
        import numpy as np
        B, T, D, E, H = (8, 512, 256, 8, 64)
        LN_EPS = 1e-05
        Bs, Ts, Ds = x.shape
        xt = x.reshape(Bs * Ts, Ds)
        logits = xt @ Wg.T
        top1 = jnp.argmax(logits, axis=-1)
        mu = jnp.mean(xt, axis=-1, keepdims=True)
        var = jnp.mean(jnp.square(xt - mu), axis=-1, keepdims=True)
        xhat = (xt - mu) * jax.lax.rsqrt(var + LN_EPS)
        n_experts = Wg.shape[0]

        def body(y, p):
            s_e, b_e, w1, bb1, w2, bb2, eid = p
            h = jax.nn.gelu((xhat * s_e + b_e) @ w1 + bb1, approximate=False)
            out = h @ w2 + bb2
            mask = (top1 == eid)[:, None].astype(out.dtype)
            return (y + mask * out, None)
        y0 = jnp.zeros_like(xt)
        y, _ = jax.lax.scan(body, y0, (ln_scale, ln_bias, W1, b1, W2, b2, jnp.arange(n_experts)))
        return y.reshape(Bs, Ts, Ds)
    x = x + _L0_xattn_ref(_layernorm(x, axis=-1), ctx_1024, L0_xattn_Wq, L0_xattn_bq, L0_xattn_Wk, L0_xattn_bk, L0_xattn_Wv, L0_xattn_bv, L0_xattn_Wo, L0_xattn_bo)
    x = x + _L0_attn_ref(_layernorm(x, axis=-1), L0_attn_wq, L0_attn_bq, L0_attn_wk, L0_attn_bk, L0_attn_wv, L0_attn_bv, L0_attn_wo, L0_attn_bo)
    x = x + _L0_ffn_ref(_layernorm(x, axis=-1), L0_ffn_gate_w, L0_ffn_gate_bias, L0_ffn_w_gate, L0_ffn_w_up, L0_ffn_w_down, L0_ffn_sh_gate, L0_ffn_sh_up, L0_ffn_sh_down)
    x = x + _L1_xattn_ref(ctx_1024, _layernorm(x, axis=-1))
    x = x + _L1_attn_ref(_layernorm(x, axis=-1), L1_attn_Wq, L1_attn_Wkv_down, L1_attn_Wk_up, L1_attn_Wv_up, L1_attn_Wout)
    x = x + _L1_ffn_ref(_layernorm(x, axis=-1), L1_ffn_Wg, L1_ffn_ln_scale, L1_ffn_ln_bias, L1_ffn_W1, L1_ffn_b1, L1_ffn_W2, L1_ffn_b2)
    return x

_drawn_inputs = setup_inputs


def setup_inputs(seed=0):
    import zlib

    import numpy as np

    out = dict(_drawn_inputs(seed))
    spreads = {'L0_xattn_bq': (0.0, 0.8),
     'L0_xattn_bk': (0.0, 2.0),
     'L0_xattn_bv': (0.0, 0.8),
     'L0_xattn_bo': (0.0, 0.8),
     'L1_ffn_ln_scale': (1.0, 0.6),
     'L1_ffn_ln_bias': (0.0, 2.0),
     'L1_ffn_b1': (0.0, 2.0),
     'L1_ffn_b2': (0.0, 2.0)}
    factors = {'L0_xattn_Wq': 8.0,
     'L0_xattn_Wk': 8.0,
     'L0_xattn_Wv': 8.0,
     'L0_xattn_Wo': 8.0,
     'L0_attn_bq': 8.0,
     'L0_attn_wk': 8.0,
     'L0_attn_bk': 8.0,
     'L0_attn_bv': 8.0,
     'L0_attn_wo': 8.0,
     'L0_attn_bo': 8.0,
     'L0_ffn_gate_w': 8.0,
     'L0_ffn_gate_bias': 8.0,
     'L0_ffn_w_gate': 8.0,
     'L0_ffn_w_up': 8.0,
     'L0_ffn_w_down': 8.0,
     'L0_ffn_sh_gate': 8.0,
     'L0_ffn_sh_up': 8.0,
     'L0_ffn_sh_down': 8.0,
     'L1_attn_Wq': 8.0,
     'L1_attn_Wkv_down': 8.0,
     'L1_attn_Wk_up': 8.0,
     'L1_attn_Wv_up': 8.0,
     'L1_attn_Wout': 8.0,
     'L1_ffn_Wg': 64.0,
     'L1_ffn_W1': 64.0,
     'L1_ffn_W2': 64.0}
    for name, (base, spread) in spreads.items():
        noise = np.random.default_rng([zlib.crc32(name.encode()), seed]).standard_normal(out[name].shape)
        drawn = base * np.exp(spread * noise) if base else spread * noise
        out[name] = jnp.asarray(drawn.astype(out[name].dtype))
    for name, factor in factors.items():
        out[name] = (out[name] * factor).astype(out[name].dtype)
    return out
```

```python
from contextlib import ExitStack

import numpy as np

import concourse.bass as bass
from concourse import mybir

F32 = mybir.dt.float32
ALU = mybir.AluOpType
ACT = mybir.ActivationFunctionType
AX = mybir.AxisListType

P = 128
D = 256
DC = D // P
NCTX = 12544

XG = 4
XH = 4
XD = 16
KT = 112
LCH = 8 * KT
NLCH = NCTX // LCH
MCH = 392
KEYS = [NCTX >> g for g in range(XG)]
KOFF = [sum(KEYS[:g]) for g in range(XG + 1)]
TILES = [k // KT for k in KEYS]
TOFF = [sum(TILES[:g]) for g in range(XG + 1)]
CLASSES = [0, 4, 2, 6, 1, 3, 5, 7]
SERVES = {r: sum(r % (1 << g) == 0 for g in range(XG)) for r in CLASSES}
SLOT = {r: sum(SERVES[q] for q in CLASSES[:n]) for n, r in enumerate(CLASSES)}
SLOTS = sum(SERVES.values())
VBANKS = [[0, 4], [2, 6, 1, 3], [5, 7]]
GROUP_TILES = [(g, c, r) for g in range(XG) for c in range(NLCH) for r in range(0, 8, 1 << g)]
UNITS = [GROUP_TILES[n:n + 2] for n in range(0, len(GROUP_TILES), 2)]
VW = XH * (XD + 1)

AH = 16
AD = 64
AW = AH * AD
AB = AW // P

NE = 32
NI = 128
NG = 8
TOPG = 4
TOPK = 8
EG = 4
SHI = 256

WB = 64
WK = 4
WU = 16
WNB = NCTX // WB
WT = WNB + WK * (P - 1)
WC = WT // WU
assert WC * WU == WT
WL = WT * WB
DCH = 448
BCH = 1792
FR = NCTX // P
BIG = 1e30
ARENA = 43200

FE = 8
FH = 64


def build_program(nc, a, upto=6):
    ctx = ExitStack()
    with ctx:
        def sb(name, shape, dt=F32):
            return ctx.enter_context(nc.sbuf_tensor(name, shape, dt))

        def sem(name):
            return ctx.enter_context(nc.semaphore(name))

        arena = sb("arena", [P, ARENA])

        def region(start, *dims, parts=P):
            n = int(np.prod(dims))
            v = arena[0:parts, start:start + n]
            if len(dims) == 2:
                v = v.rearrange("p (a b) -> p a b", a=dims[0])
            if len(dims) == 3:
                v = v.rearrange("p (a b c) -> p a b c", a=dims[0], b=dims[1])
            return v

        rows = [sb("rows_even", [P, D]), sb("rows_odd", [P, D])]
        x = [rows[k % 2] for k in range(7)]
        ident = sb("ident", [P, P])
        eps = sb("eps", [P, 1])
        ln_out = sb("ln_out", [P, D])
        ln_outT = sb("ln_outT", [P, DC, P])
        ln_stats = sb("ln_stats", [P, 16])
        small = sb("small", [P, LCH])
        bank = ctx.enter_context(nc.psum_tensor("bank", [P, 8, 512], F32))

        keysT = [region(KOFF[g], KEYS[g]) for g in range(XG)]
        vals = region(KOFF[4], NLCH, SLOTS * VW, parts=KT)
        at = KOFF[4] + TOFF[4] * VW
        ctxT = [region(at + s * DC * LCH, DC, LCH) for s in range(2)]
        squares = region(at + 2 * DC * LCH, DC, LCH)
        assert at + 3 * DC * LCH <= ARENA
        probs = [region(at + s * 1024, 2, 512, parts=KT) for s in range(3)]
        w_kq = sb("w_kq", [P, 4, XG * P])
        w_k, w_q = w_kq[:, 0:2, :], w_kq[:, 2:4, :]
        query_blocks = w_kq
        w_v = sb("w_v", [P, DC, XG * VW])
        w_o = sb("w_o", [P, DC, D])
        b_k = sb("b_k", [P, XG])
        b_q = sb("b_q", [P, XG])
        b_v = sb("b_v", [KT, SLOTS * VW])
        b_o = sb("b_o", [P, D])
        ones_col = sb("ones_col", [P, 1])
        norms_row = [sb("norms_row", [1, LCH]), small[0:1, :]]
        queriesT = sb("queriesT", [P, XG, P])
        maxes = small[:, 0:60 * 4].rearrange("p (n a) -> p n a", a=XH)
        MOFF = [sum(KEYS[:g]) // MCH for g in range(XG + 1)]
        neg_max = region(at + 3072, XG * P)
        att_sums = [region(at + 3584 + 512 * s, 512, parts=VW) for s in range(2)]
        xo = ln_out
        xoT = ln_outT


        AW2 = DC * AW
        wa_q = region(0, DC, AW)
        wa_k = region(AW2, DC, AW)
        wa_v = region(2 * AW2, DC, AW)
        wa_o = region(3 * AW2, AB, D)
        ba = region(4 * AW2, 3, AW)
        ba_o = region(4 * AW2 + 3 * AW, D)
        rope_cos = region(4 * AW2 + 3 * AW + D, AD)
        rope_sin = region(4 * AW2 + 3 * AW + D + AD, AD)
        lat_q = region(37632, DC, AW)
        lat_o = region(37632 + AW2, AB, D)
        lat_down = region(37632 + 2 * AW2, DC, AD)
        lat_up = region(32000, 2, 512)
        lat_up_v = region(33024, 2, 512)
        latT = region(34048, P)
        work = KOFF[1]
        proj = [region(work + n * AW, AW) for n in range(3)]
        rope_tmp = region(work + 3 * AW, AW)
        qkT = [region(work + (4 + n) * AW, AB, P) for n in range(2)]
        scores_sb = region(work + 6 * AW, AH, P)
        probsT = region(work + 8 * AW, AH, P)
        heads_out = region(work + 10 * AW, AW)
        heads_outT = region(work + 11 * AW, AB, P)
        row_max = small[:, 288:304]
        row_sum = small[:, 304:320]
        causal = sb("causal", [P, P])

        LOTS = NE // EG + 1
        lot_at = [work + 12 * AW + n * 3072 for n in range(5)] + [n * 3072 for n in range(4)]
        lot_num = [EG] * (LOTS - 1) + [SHI // NI]
        lot_gate = [region(lot_at[n], DC, lot_num[n] * NI) for n in range(LOTS)]
        lot_up = [region(lot_at[n] + 1024, DC, lot_num[n] * NI) for n in range(LOTS)]
        lot_down = [region(lot_at[n] + 2048, lot_num[n], D) for n in range(LOTS)]
        gate_w = region(work, DC, NE)
        gate_b = region(work + 64, NE)
        lower = region(work + 96, NE, NE)
        pair_gt = region(work + 96 + 1024, NE, NE)
        pair_eq = region(work + 96 + 2048, NE, NE)
        r_at = work + 96 + 3072
        r_scores, r_biased, r_masked, r_rank, r_sel = [region(r_at + 32 * n, NE) for n in range(5)]
        r_pairs = region(r_at + 160, NG, 6)
        r_group, r_grank = region(r_at + 208, NG), region(r_at + 216, NG)
        r_sum = region(r_at + 224, 2)
        combine = region(r_at + 226, NE + 2)
        act_gate = [region(r_at + 512 + 512 * n, 512) for n in range(2)]
        act_h = [region(r_at + 1536 + 512 * n, 512) for n in range(2)]
        act_hT = [region(r_at + 2560 + 512 * n, EG, P) for n in range(2)]
        assert r_at + 3584 <= work + 12 * AW

        ctx_rows = region(0, FR, D)
        dtw = FR * D
        dist_ring = [region(dtw + n * WU * WB, WU * WB) for n in range(4)]
        cost_ring = region(dtw + 4096, 1 + 4 * WU * WB)
        pair_ring = [region(dtw + 8200 + WB * n, WB) for n in range(4)]
        ctxT_ring = [region(dtw + 8500 + 896 * n, DC, DCH) for n in range(4)]
        norm_ring = [region(dtw + 8500 + 3584 + 448 * n, DCH, parts=1) for n in range(4)]
        dist_tmp = [region(dtw + 13900 + 448 * n, DCH) for n in range(2)]
        dist_out = [region(dtw + 14800 + 448 * n, DCH) for n in range(4)]
        xm2T = sb("xm2T", [P, DC, P])
        x_norm = sb("x_norm", [P, 1])
        shift = sb("shift", [P, P])
        ones = sb("ones", [P, P])
        ones_row = sb("ones_row", [1, P])
        rows_i = sb("rows_i", [P, FR])
        own = region(dtw, BCH + 1)
        left = region(dtw + 1793, BCH + 1)
        dist_c = region(dtw + 3586, BCH + 1)
        up_lt, up_le, diag, step_one, deltas = [region(dtw + 5380 + BCH * n, BCH) for n in range(5)]
        deltas_x = region(dtw, P, FR)
        MF = 14
        masks = [region(dtw + P * FR + n * MF * P, MF, P) for n in range(1)]
        bounds = region(dtw + P * FR + MF * P + 64, P + 1)
        picked = region(dtw + P * FR + MF * P + 256, FR)
        picked_sum = region(dtw + P * FR + MF * P + 400, P)

        f_w1 = region(0, DC, FE * FH)
        f_w2 = region(1024, FE, D, parts=FH + 1)
        f_g = region(3072, DC, FE)
        f_s = region(3088, DC, FE)
        f_b = region(3104, DC, FE)
        f_b1 = region(3120, FE, parts=FH)
        f_ramp = region(3128, FE)
        f_logit, f_val, f_mask = [region(3136 + 8 * n, FE) for n in range(3)]
        f_max = region(3160, 2)
        f_xT = [region(3200 + 256 * n, DC, P) for n in range(2)]
        f_hT = [region(3712 + 128 * n, P, parts=FH + 1) for n in range(2)]

        dist_d = nc.dram_tensor("dist_d", [P, NCTX], F32, kind="Internal").ap()
        cost_d = nc.dram_tensor("cost_d", [P, WL], F32, kind="Internal").ap()
        delta_d = nc.dram_tensor("delta_d", [P, NCTX], F32, kind="Internal").ap()
        norms_d = nc.dram_tensor("norms_d", [1, NCTX], F32, kind="Internal").ap()

        S = {}

        def signal(*names):
            for n in names:
                S[n] = sem(n)

        signal("const_in", "x_in", "xw_in")
        signal("ln_var", "ln_std", "ln_rows", "ln_turned", "ln_ready")
        signal("dve_chain", "act_chain")
        signal("ctxT_in0", "ctxT_in1", "ctxT_used", "squares_ready", "squares_used",
               "kproj_ready", "kproj_taken", "vproj_ready", "vproj_taken", "norms_stored0", "norms_stored1",
               "q_ready", "q_taken", "max_scores", "max_taken", "negmax_ready", "negmax_turned",
               "qmax_ready", "q_blocks", "scores_ready", "scores_taken", "probs_ready", "probs_used",
               "att_ready", "att_copied", "att_turned", "xo_ready", "xo_turned", "xoT_ready",
               "x_proj", "x_done", "out_stored")

        for z in range(2):
            signal(*[f"{n}{z}" for n in (
                "wa_in", "a_proj", "a_rows", "a_turned", "a_qkT", "a_scores", "a_shifted", "a_probs", "a_probs_turned",
                "a_probsT", "a_values", "a_heads", "a_heads_turned", "a_headsT", "a_out")])
        signal("lat_turned", "latT_ready")
        signal("rout_in", "lots_in0", "lots_in1", "r_logits", "r_sigmoid", "r_biased", "r_combine", "e_up", "e_silu", "e_h", "e_turned", "e_hT", "e_out")
        signal("dist_w", "xnorm_ready", "xm2T_ready", "dist_sum", "dist_relu", "dist_sqrt",
               *[f"dchunk_in{n}" for n in range(4)], *[f"dist_stored{n}" for n in range(4)],
               *[f"dist_in{n}" for n in range(4)], *[f"cost_stored{n}" for n in range(4)],
               "scan_done", "pairs_ready", "shifted", "wrapped", "ctx_in", "own_in", "choice_done", "deltas_stored",
               "deltas_x_in", "picked_ready", "bound_ready", "bounds_ready", "masks_ready", "masks_used", "expanded")
        signal("f_in", "f_logits", "f_xT_ready", "f_h", "f_hT_ready", "f_out", "f_added", "x_out")

        def flat(v):
            return v.rearrange("p a b -> p (a b)")

        def skewed(t, pitch, first, start, num, parts=P):
            return bass.AP(tensor=t.tensor, offset=first + start, ap=[[pitch, parts], [1, num]])

        block = ctx.enter_context(nc.Block())

        @block.sync
        def _(sp):
            sp.dma_start(x[0][:, :], a["x"]).then_inc(S["x_in"], 16)
            sp.dma_start(ident[:, :], a["ident"]).then_inc(S["const_in"], 16)
            sp.dma_start(causal[:, :], a["causal"]).then_inc(S["const_in"], 16)
            sp.dma_start(shift[:, :], a["shift"]).then_inc(S["const_in"], 16)
            sp.dma_start(rows_i[:, :], a["rows_i"]).then_inc(S["const_in"], 16)
            for t, n in ((w_k, "xw_k"), (w_q, "xw_q"), (w_v[:, :, :], "xw_v"), (w_o[:, :, :], "xw_o")):
                sp.dma_start(t, a[n].rearrange("(c p) n -> p c n", p=P)).then_inc(S["xw_in"], 16)
            sp.dma_start(b_k[:, :], a["xb_k"]).then_inc(S["xw_in"], 16)
            sp.dma_start(b_q[:, :], a["xb_q"]).then_inc(S["xw_in"], 16)
            sp.dma_start(b_v[:, :], a["xb_v"].broadcast_to((KT, SLOTS * VW))).then_inc(S["xw_in"], 16)
            sp.dma_start(b_o[:, :], a["xb_o"].broadcast_to((P, D))).then_inc(S["xw_in"], 16)
            src = a["ctxT"].rearrange("(c p) n -> p c n", p=P)
            for n in range(2):
                sp.dma_start(ctxT[n], src[:, :, n * LCH:(n + 1) * LCH]).then_inc(S[f"ctxT_in{n}"], 16)
            with sp.Fori(1, NLCH // 2) as i:
                for n in range(2):
                    sp.wait_ge(S["vproj_ready"], i * 10 + (5 * n - 6))
                    sp.wait_ge(S["squares_ready"], i * 2 + (n - 1))
                    sp.dma_start(ctxT[n], src[:, :, bass.ds(i * (2 * LCH) + n * LCH, LCH)]).then_inc(S[f"ctxT_in{n}"], 16)
                    sp.wait_ge(S["vproj_taken"], i * 10 + 5 * n)
                    sp.dma_start(norms_d[0:1, bass.ds(i * (2 * LCH) + (n - 2) * LCH, LCH)], norms_row[n][0:1, :]).then_inc(S[f"norms_stored{n}"], 16)
            for n in range(2):
                sp.wait_ge(S["vproj_taken"], 5 * (NLCH + n))
                sp.dma_start(norms_d[0:1, (NLCH - 2 + n) * LCH:(NLCH - 1 + n) * LCH], norms_row[n][0:1, :]).then_inc(S[f"norms_stored{n}"], 16)
            if upto >= 2:
                sp.wait_ge(S["probs_used"], TILES[0] // 2)
                for t, n in ((wa_q, "aw_q"), (wa_k, "aw_k"), (wa_v, "aw_v")):
                    sp.dma_start(t, a[n].rearrange("(c p) n -> p c n", p=P)).then_inc(S["wa_in0"], 16)
                sp.dma_start(wa_o, a["aw_o"].rearrange("(c p) n -> p c n", p=P)).then_inc(S["wa_in0"], 16)
                for m, n in enumerate(("ab_q", "ab_k", "ab_v")):
                    sp.dma_start(ba[:, m, :], a[n].broadcast_to((P, AW))).then_inc(S["wa_in0"], 16)
                sp.dma_start(ba_o, a["ab_o"].broadcast_to((P, D))).then_inc(S["wa_in0"], 16)
                sp.dma_start(rope_cos, a["rope_cos"]).then_inc(S["wa_in0"], 16)
                sp.dma_start(rope_sin, a["rope_sin"]).then_inc(S["wa_in0"], 16)
            if upto >= 3:
                def load_lot(n, s_in):
                    w = lot_num[n] * NI
                    for t, m in ((lot_gate, "gate"), (lot_up, "up")):
                        src = a["ew_" + m][:, n * EG * NI:n * EG * NI + w] if n < LOTS - 1 else a["esh_" + m]
                        sp.dma_start(t[n], src.rearrange("(c p) n -> p c n", p=P)).then_inc(S[s_in], 16)
                    src = a["ew_down"][:, n * EG:(n + 1) * EG, :] if n < LOTS - 1 else a["esh_down"].rearrange("(c p) n -> p c n", p=P)
                    sp.dma_start(lot_down[n], src).then_inc(S[s_in], 16)

                sp.wait_ge(S["x_done"], 1)
                for n in range(5):
                    load_lot(n, "lots_in0")
                sp.wait_ge(S["x_done"], 2)
                sp.dma_start(gate_w, a["rw"].rearrange("(c p) n -> p c n", p=P)).then_inc(S["rout_in"], 16)
                sp.dma_start(gate_b, a["rb"].broadcast_to((P, NE))).then_inc(S["rout_in"], 16)
                sp.dma_start(flat(lower), a["lower"].broadcast_to((P, NE * NE))).then_inc(S["rout_in"], 16)
                for n in range(5, LOTS):
                    load_lot(n, "lots_in1")
            if upto >= 4:
                sp.wait_ge(S["x_done"], 3)
                srcT = a["ctxT"].rearrange("(c p) n -> p c n", p=P)
                for n in range(NCTX // DCH):
                    s = n % 4
                    if n >= 4:
                        sp.wait_ge(S["dist_sum"], n - 3)
                    sp.dma_start(ctxT_ring[s], srcT[:, :, n * DCH:(n + 1) * DCH]).then_inc(S[f"dchunk_in{s}"], 16)
                    sp.dma_start(norm_ring[s], norms_d[0:1, n * DCH:(n + 1) * DCH]).then_inc(S[f"dchunk_in{s}"], 16)
                    if n >= 2:
                        sp.wait_ge(S["dist_sqrt"], n - 1)
                        sp.dma_start(dist_d[:, (n - 2) * DCH:(n - 1) * DCH], dist_out[(n - 2) % 4]).then_inc(S[f"dist_stored{(n - 2) % 4}"], 16)
                for n in range(NCTX // DCH - 2, NCTX // DCH):
                    sp.wait_ge(S["dist_sqrt"], n + 1)
                    sp.dma_start(dist_d[:, n * DCH:(n + 1) * DCH], dist_out[n % 4]).then_inc(S[f"dist_stored{n % 4}"], 16)
                for n in range(4):
                    sp.wait_ge(S[f"dist_stored{n}"], 16 * (NCTX // DCH // 4))
                CH = WU * WB
                src = skewed(dist_d, NCTX - WK * WB, 0, 0, WL)
                for n in range(4):
                    sp.dma_start(dist_ring[n], src[:, n * CH:(n + 1) * CH]).then_inc(S[f"dist_in{n}"], 16)
                sp.dma_start(ctx_rows, a["ctx"].rearrange("(p f) n -> p f n", f=FR)).then_inc(S["ctx_in"], 16)
                with sp.Fori(0, WC // 4 - 1) as i:
                    for n in range(4):
                        sp.wait_ge(S["scan_done"], i * (4 * WU) + ((n + 1) * WU + 1))
                        sp.dma_start(cost_d[:, bass.ds(i * (4 * CH) + n * CH, CH)], cost_ring[:, 1 + n * CH:1 + (n + 1) * CH]).then_inc(S[f"cost_stored{n}"], 16)
                        sp.dma_start(dist_ring[n], src[:, bass.ds(i * (4 * CH) + (n + 4) * CH, CH)]).then_inc(S[f"dist_in{n}"], 16)
                for n in range(4):
                    sp.wait_ge(S["scan_done"], (WC - 4 + n + 1) * WU + 1)
                    sp.dma_start(cost_d[:, (WC - 4 + n) * CH:(WC - 3 + n) * CH], cost_ring[:, 1 + n * CH:1 + (n + 1) * CH]).then_inc(S[f"cost_stored{n}"], 16)
                for n in range(4):
                    sp.wait_ge(S[f"cost_stored{n}"], 16 + 16 * (WC // 4))
                for n in range(NCTX // BCH):
                    if n >= 1:
                        sp.wait_ge(S["choice_done"], n + 1)
                    lo = 1 if n == 0 else 0
                    pitch = WL + WK * WB
                    first = n * BCH - 1 + lo
                    sp.dma_start(own[:, lo:BCH + 1], skewed(cost_d, pitch, 0, first, BCH + 1 - lo)).then_inc(S["own_in"], 16)
                    sp.dma_start(left[1:P, lo:BCH + 1], skewed(cost_d, pitch, 0, first, BCH + 1 - lo, P - 1)).then_inc(S["own_in"], 16)
                    if n >= 1:
                        sp.dma_start(delta_d[:, (n - 1) * BCH:n * BCH], deltas).then_inc(S["deltas_stored"], 16)
                n = NCTX // BCH
                sp.wait_ge(S["choice_done"], n + 1)
                sp.dma_start(delta_d[:, (n - 1) * BCH:n * BCH], deltas).then_inc(S["deltas_stored"], 16)
                sp.wait_ge(S["deltas_stored"], 16 * n)
                sp.dma_start(deltas_x, delta_d.rearrange("j (p f) -> p j f", f=FR)).then_inc(S["deltas_x_in"], 16)
            if upto >= 5:
                sp.wait_ge(S["x_done"], 4)
                sp.dma_start(lat_q, a["lw_q"].rearrange("(c p) n -> p c n", p=P)).then_inc(S["wa_in1"], 16)
                sp.dma_start(lat_o, a["lw_o"].rearrange("(c p) n -> p c n", p=P)).then_inc(S["wa_in1"], 16)
                sp.dma_start(lat_down, a["lw_down"].rearrange("(c p) n -> p c n", p=P)).then_inc(S["wa_in1"], 16)
                for n, m in enumerate(("lw_k", "lw_v")):
                    sp.dma_start(lat_up[0:AD, :, :] if n == 0 else lat_up_v[0:AD, :, :], a[m].rearrange("p (a n) -> p a n", a=2)).then_inc(S["wa_in1"], 16)
            if upto >= 6:
                sp.dma_start(f_w1, a["fw1"].rearrange("(c p) n -> p c n", p=P)).then_inc(S["f_in"], 16)
                sp.dma_start(f_w2, a["fw2"]).then_inc(S["f_in"], 16)
                for t, m in ((f_g, "fg"), (f_s, "fs"), (f_b, "fb")):
                    sp.dma_start(t, a[m].rearrange("(c p) n -> p c n", p=P)).then_inc(S["f_in"], 16)
                sp.dma_start(f_b1, a["fb1"]).then_inc(S["f_in"], 16)
                sp.dma_start(f_ramp, a["ramp"].broadcast_to((P, FE))).then_inc(S["f_in"], 16)
            for n in range(2):
                sp.wait_ge(S[f"norms_stored{n}"], 16 + 8 * NLCH)
            sp.wait_ge(S["x_done"], upto)
            sp.dma_start(a["out"], x[upto][:, :]).then_inc(S["x_out"], 16)
            sp.wait_ge(S["x_out"], 16)

        @block.gpsimd
        def _(pool):
            for n in range(2):
                pool.wait_ge(S[f"ctxT_in{n}"], 16)
                if n == 1:
                    pool.wait_ge(S["vproj_ready"], 5)
                nc.gpsimd.tensor_tensor(squares, ctxT[n], ctxT[n], ALU.mult).then_inc(S["squares_ready"], 1)
            with pool.Fori(1, NLCH // 2) as i:
                for n in range(2):
                    pool.wait_ge(S[f"ctxT_in{n}"], i * 16 + 16)
                    pool.wait_ge(S["vproj_ready"], i * 10 + 5 * n)
                    nc.gpsimd.tensor_tensor(squares, ctxT[n], ctxT[n], ALU.mult).then_inc(S["squares_ready"], 1)

        @block.scalar
        def _(act):
            def ln_std(k):
                act.wait_ge(S["ln_var"], k + 1)
                nc.scalar.activation(ln_stats[:, 14:15], ln_stats[:, 13:14], ACT.Sqrt, bias=eps[:, 0:1]).then_inc(S["ln_std"], 1)

            act.sem_inc(S["kproj_taken"], 4)
            act.wait_ge(S["xw_in"], 16 * 8)
            with act.Fori(0, NLCH // 2) as i:
                for n in range(2):
                    for m in range(4):
                        act.wait_ge(S["kproj_ready"], i * 8 + (4 * n + m + 1))
                        if m < 2:
                            dst = keysT[0][:, bass.ds(i * (2 * LCH) + (n * LCH + m * 448), 448)]
                            nc.scalar.activation(dst, bank[:, m, 0:448], ACT.Identity, bias=b_k[:, 0:1]).then_inc(S["kproj_taken"], 1)
                        elif m == 2:
                            dst = keysT[1][:, bass.ds(i * LCH + n * (LCH // 2), LCH // 2)]
                            nc.scalar.activation(dst, bank[:, 2, 0:448], ACT.Identity, bias=b_k[:, 1:2]).then_inc(S["kproj_taken"], 1)
                        else:
                            dst = keysT[2][:, bass.ds(i * (LCH // 2) + n * (LCH // 4), LCH // 4)]
                            nc.scalar.activation(dst, bank[:, 3, 0:224], ACT.Identity, bias=b_k[:, 2:3])
                            dst = keysT[3][:, bass.ds(i * (LCH // 4) + n * (LCH // 8), LCH // 8)]
                            nc.scalar.activation(dst, bank[:, 3, 224:336], ACT.Identity, bias=b_k[:, 3:4]).then_inc(S["kproj_taken"], 1)
            ln_std(0)
            for u in range(len(UNITS)):
                s = u % 3
                act.wait_ge(S["scores_ready"], u + 1)
                if u >= 3:
                    act.wait_ge(S["probs_used"], u - 2)
                nc.scalar.activation(probs[s], bank[0:KT, 2 * s:2 * s + 2, :], ACT.Exp, scale=XD ** -0.5).then_inc(S["probs_ready"], 1)

            def attention(z, k):
                ln_std(k)
                for n in range(2):
                    act.wait_ge(S[f"a_turned{z}"], n + 1)
                    nc.scalar.activation(flat(qkT[n]), flat(bank[:, 2 * n:2 * n + 2, :]), ACT.Copy).then_inc(S[f"a_qkT{z}"], 1)
                for n in range(4):
                    act.wait_ge(S[f"a_shifted{z}"], n + 1)
                    nc.scalar.activation(scores_sb[:, 4 * n:4 * n + 4, :], scores_sb[:, 4 * n:4 * n + 4, :], ACT.Exp, scale=AD ** -0.5).then_inc(S[f"a_probs{z}"], 1)
                for n in range(4):
                    act.wait_ge(S[f"a_probs_turned{z}"], n + 1)
                    nc.scalar.activation(flat(probsT[:, 4 * n:4 * n + 4, :]), bank[:, n, :], ACT.Copy).then_inc(S[f"a_probsT{z}"], 1)
                act.wait_ge(S[f"a_heads_turned{z}"], 1)
                nc.scalar.activation(flat(heads_outT), flat(bank[:, 0:2, :]), ACT.Copy).then_inc(S[f"a_headsT{z}"], 1)

            if upto >= 2:
                attention(0, 1)
            if upto >= 3:
                ln_std(2)
                act.wait_ge(S["r_logits"], 1)
                nc.scalar.activation(r_scores, bank[:, 4, 0:NE], ACT.Sigmoid).then_inc(S["r_sigmoid"], 1)

                def silu(n):
                    w = lot_num[n] * NI
                    act.wait_ge(S["e_up"], n + 1)
                    if n >= 2:
                        act.wait_ge(S["e_h"], n - 1)
                    nc.scalar.activation(act_gate[n % 2][:, 0:w], bank[:, 2 * (n % 2), 0:w], ACT.Silu).then_inc(S["e_silu"], 1)

                def copy_hT(n):
                    act.wait_ge(S["e_turned"], n + 1)
                    if n >= 2:
                        act.wait_ge(S["e_out"], n - 1)
                    nc.scalar.activation(flat(act_hT[n % 2][:, 0:lot_num[n], :]), bank[:, 4 + n % 2, 0:lot_num[n] * NI], ACT.Copy).then_inc(S["e_hT"], 1)

                for n in range(LOTS):
                    silu(n)
                    if n >= 1:
                        copy_hT(n - 1)
                copy_hT(LOTS - 1)
            if upto >= 4:
                ln_std(3)
                act.wait_ge(S["ln_rows"], 4)
                act.wait_ge(S["xm2T_ready"], 1)
                nc.scalar.activation(dist_tmp[0][:, 0:D], ln_out[:, :], ACT.Square, accum_out=x_norm[:, 0:1]).then_inc(S["xnorm_ready"], 1)
                act.wait_ge(S["xnorm_ready"], 1)
                for n in range(NCTX // DCH):
                    act.wait_ge(S["dist_sum"], n + 1)
                    if n >= 2:
                        act.wait_ge(S["dist_sqrt"], n - 1)
                    nc.scalar.activation(dist_tmp[n % 2], bank[:, n % 4, 0:DCH], ACT.Relu, bias=x_norm[:, 0:1]).then_inc(S["dist_relu"], 1)
                    act.wait_ge(S["dist_relu"], n + 1)
                    if n >= 4:
                        act.wait_ge(S[f"dist_stored{n % 4}"], 16 * (n // 4))
                    nc.scalar.activation(dist_out[n % 4], dist_tmp[n % 2], ACT.Sqrt).then_inc(S["dist_sqrt"], 1)
            if upto >= 5:
                attention(1, 4)
            if upto >= 6:
                ln_std(5)
                ln_std(6)
                for e in range(FE):
                    act.wait_ge(S["f_h"], e + 1)
                    if e >= 2:
                        act.wait_ge(S["f_out"], e - 1)
                    nc.scalar.activation(f_hT[e % 2][0:FH, :], bank[0:FH, e % 2, 0:P], ACT.Gelu, bias=f_b1[:, e:e + 1]).then_inc(S["f_hT_ready"], 1)

        @block.vector
        def _(dve):
            chain = [0]

            def link(ins):
                chain[0] += 1
                ins.then_inc(S["dve_chain"], 1)
                dve.wait_ge(S["dve_chain"], chain[0])

            def layer_norm(k, rows):
                link(nc.vector.bn_stats(ln_stats[:, 0:6], rows[:, :]))
                nc.vector.bn_aggr(ln_stats[:, 12:14], ln_stats[:, 0:6]).then_inc(S["ln_var"], 1)
                dve.wait_ge(S["ln_std"], k + 1)
                link(nc.vector.reciprocal(ln_stats[:, 15:16], ln_stats[:, 14:15]))
                nc.vector.tensor_scalar(ln_out[:, :], rows[:, :], ln_stats[:, 12:13], ln_stats[:, 15:16],
                                        ALU.subtract, ALU.mult).then_inc(S["ln_rows"], 1)
                dve.wait_ge(S["ln_turned"], k + 1)
                nc.vector.tensor_copy(ln_outT[:, :, :], bank[:, 7, 0:D].rearrange("p (c q) -> p c q", c=DC)).then_inc(S["ln_ready"], 1)

            dve.sem_inc(S["vproj_taken"], 5)
            dve.sem_inc(S["norms_stored0"], 16)
            dve.sem_inc(S["norms_stored1"], 16)
            nc.vector.memset(eps[:, :], 1e-5)
            nc.vector.memset(ones_row[:, :], 1.0)
            nc.vector.memset(ones_col[:, :], 1.0).then_inc(S["q_taken"], 1)
            dve.wait_ge(S["xw_in"], 16 * 8)

            def norms(i, n, m):
                if m == 0:
                    dve.wait_ge(S[f"norms_stored{n}"], i * 16 + 16)
                nc.vector.tensor_copy(norms_row[n][0:1, m * 448:(m + 1) * 448], bank[0:1, 7, 0:448]).then_inc(S["vproj_taken"], 1)

            with dve.Fori(0, NLCH // 2) as i:
                for n in range(2):
                    dve.wait_ge(S["vproj_ready"], i * 10 + (5 * n + 1))
                    norms(i, n, 0)
                    for m, classes in enumerate(VBANKS):
                        dve.wait_ge(S["vproj_ready"], i * 10 + (5 * n + 2 + m))
                        lo, hi = SLOT[classes[0]] * VW, (SLOT[classes[-1]] + SERVES[classes[-1]]) * VW
                        nc.vector.tensor_tensor(vals[:, bass.ds(i * 2 + n, 1), lo:hi].rearrange("p a n -> p (a n)"),
                                                bank[0:KT, 4 + m, 0:hi - lo], b_v[:, lo:hi], ALU.add).then_inc(S["vproj_taken"], 1)
                    dve.wait_ge(S["vproj_ready"], i * 10 + (5 * n + 5))
                    norms(i, n, 1)
            dve.wait_ge(S["x_in"], 16)
            layer_norm(0, x[0])
            dve.wait_ge(S["q_ready"], 1)
            for g in range(XG):
                last = nc.vector.tensor_scalar(queriesT[:, g, :], bank[:, 0, g * P:(g + 1) * P], b_q[:, g:g + 1], None, ALU.add)
            last.then_inc(S["q_taken"], 1)
            link(nc.vector.memset(query_blocks[:, :, :], 0.0))
            dve.wait_ge(S["q_taken"], 2)
            for h in range(XH):
                last = nc.vector.tensor_copy(query_blocks[32 * h:32 * h + 32, :, h * P:(h + 1) * P], queriesT[32 * h:32 * h + 32, :, :])
            last.then_inc(S["q_blocks"], 1)
            nc.vector.memset(neg_max, 0.0)
            dve.wait_ge(S["norms_stored1"], 16 + 8 * NLCH)
            for n in range(MOFF[4]):
                s = n % 2
                dve.wait_ge(S["max_scores"], n + 1)
                last = nc.vector.tensor_reduce(maxes[:, n, :], bank[:, 4 * s:4 * s + 4, 0:MCH], AX.X, ALU.max)
                last.then_inc(S["max_taken"], 1)
            dve.wait_ge(S["max_taken"], MOFF[4])
            for g in range(XG):
                link(nc.vector.tensor_reduce(small[:, 256 + 4 * g:260 + 4 * g],
                                             maxes[:, MOFF[g]:MOFF[g + 1], :].rearrange("p n a -> p a n"), AX.X, ALU.max))
            nc.vector.tensor_scalar(neg_max.rearrange("p (g a c) -> p g a c", g=XG, a=XH)[:, :, :, XD:XD + 1],
                                    small[:, 256:272].rearrange("p (g a o) -> p g a o", g=XG, a=XH),
                                    -1.0, None, ALU.mult).then_inc(S["negmax_ready"], 1)
            dve.wait_ge(S["negmax_turned"], 1)
            for h in range(XH):
                q = query_blocks[32 * h:32 * h + 32, :, h * P:(h + 1) * P]
                last = nc.vector.tensor_tensor(q, q, bank[32 * h:32 * h + 32, 0, :].rearrange("p (g q) -> p g q", g=XG), ALU.add)
            last.then_inc(S["qmax_ready"], 1)
            for g in range(XG):
                dve.wait_ge(S["probs_used"], TOFF[g + 1] // 2)
                if g >= 2:
                    dve.wait_ge(S["att_turned"], g - 1)
                nc.vector.tensor_copy(att_sums[g % 2], bank[0:VW, 6 + g % 2, :]).then_inc(S["att_copied"], 1)
            dve.wait_ge(S["att_turned"], XG)
            rsum = small[:, 272:288].rearrange("p (g h o) -> p g h o", g=XG, h=XH)
            att = bank[:, 0:4, 0:XH * VW].rearrange("p g (h n) -> p g h n", h=XH)
            for g in range(XG):
                for h in range(XH):
                    link(nc.vector.reciprocal(rsum[:, g, h], att[:, g, h, h * (XD + 1) + XD:(h + 1) * (XD + 1)]))
            xo_v = xo[:, :].rearrange("p (h g c) -> p g h c", g=XG, h=XH)
            for g in range(XG):
                for h in range(XH):
                    last = nc.vector.tensor_scalar(xo_v[:, g, h], att[:, g, h, h * (XD + 1):h * (XD + 1) + XD], rsum[:, g, h], None, ALU.mult)
            last.then_inc(S["xo_ready"], 1)
            dve.wait_ge(S["xo_turned"], 1)
            nc.vector.tensor_copy(xoT[:, :, :], bank[:, 5, 0:D].rearrange("p (c q) -> p c q", c=DC)).then_inc(S["xoT_ready"], 1)
            dve.wait_ge(S["x_proj"], 1)
            link(nc.vector.tensor_tensor(x[1][:, :], bank[:, 4, 0:D], b_o[:, :], ALU.add))
            nc.vector.tensor_tensor(x[1][:, :], x[1][:, :], x[0][:, :], ALU.add).then_inc(S["x_done"], 1)

            def attention(z, k, bias_out):
                layer_norm(k, x[k])
                dve.wait_ge(S[f"wa_in{z}"], 16 * (10 if z == 0 else 5))
                if z == 1:
                    dve.wait_ge(S["lat_turned"], 1)
                    nc.vector.tensor_copy(latT[0:AD, :], bank[0:AD, 6, 0:P]).then_inc(S["latT_ready"], 1)
                for n in range(3):
                    dve.wait_ge(S[f"a_proj{z}"], n + 1)
                    src = flat(bank[:, 2 * n:2 * n + 2, :])
                    if z == 1:
                        nc.vector.tensor_copy(proj[n], src).then_inc(S[f"a_rows{z}"], 1)
                    elif n == 2:
                        nc.vector.tensor_tensor(proj[n], src, ba[:, n, :], ALU.add).then_inc(S[f"a_rows{z}"], 1)
                    else:
                        link(nc.vector.tensor_tensor(proj[n], src, ba[:, n, :], ALU.add))
                        v = proj[n].rearrange("p (h i t) -> p h i t", i=AD // 2, t=2)
                        tmp = rope_tmp.rearrange("p (h i t) -> p h i t", i=AD // 2, t=2)
                        sin = rope_sin.rearrange("p (o i t) -> p o i t", o=1, t=2)
                        for t in range(2):
                            last = nc.vector.tensor_tensor(tmp[:, :, :, t], v[:, :, :, 1 - t], sin[:, :, :, t].broadcast_to((P, AH, AD // 2)), ALU.mult)
                        link(last)
                        v = proj[n].rearrange("p (h i) -> p h i", i=AD)
                        link(nc.vector.tensor_tensor(v, v, rope_cos.rearrange("p (o i) -> p o i", o=1).broadcast_to((P, AH, AD)), ALU.mult))
                        nc.vector.tensor_tensor(proj[n], proj[n], rope_tmp, ALU.add).then_inc(S[f"a_rows{z}"], 1)
                if z == 0:
                    dve.wait_ge(S["const_in"], 64)
                for n in range(4):
                    c = scores_sb[:, 4 * n:4 * n + 4, :]
                    dve.wait_ge(S[f"a_scores{z}"], n + 1)
                    link(nc.vector.tensor_tensor(c, bank[:, 4 + n, :].rearrange("p (s q) -> p s q", s=4),
                                                 causal[:, :].rearrange("p (o q) -> p o q", o=1).broadcast_to((P, 4, P)), ALU.add))
                    link(nc.vector.tensor_reduce(row_max[:, 4 * n:4 * n + 4], c, AX.X, ALU.max))
                    nc.vector.tensor_tensor(c, c, row_max[:, 4 * n:4 * n + 4].rearrange("p (s o) -> p s o", o=1).broadcast_to((P, 4, P)),
                                            ALU.subtract).then_inc(S[f"a_shifted{z}"], 1)
                for n in range(4):
                    dve.wait_ge(S[f"a_probs{z}"], n + 1)
                    link(nc.vector.tensor_reduce(row_sum[:, 4 * n:4 * n + 4], scores_sb[:, 4 * n:4 * n + 4, :], AX.X, ALU.add))
                link(nc.vector.reciprocal(row_sum, row_sum))
                inv = row_sum.rearrange("p (r b o) -> p b r o", r=2, o=1)
                for n in range(2):
                    dve.wait_ge(S[f"a_values{z}"], 4)
                    last = nc.vector.tensor_tensor(heads_out[:, n * 512:(n + 1) * 512].rearrange("p (b r i) -> p b r i", b=4, r=2),
                                                   bank[:, 4 + n, :].rearrange("p (b r i) -> p b r i", b=4, r=2),
                                                   inv[:, 4 * n:4 * n + 4].broadcast_to((P, 4, 2, AD)), ALU.mult)
                last.then_inc(S[f"a_heads{z}"], 1)
                dve.wait_ge(S[f"a_out{z}"], 1)
                if z == 0:
                    link(nc.vector.tensor_tensor(heads_out[:, 0:D], bank[:, 2, 0:D], ba_o, ALU.add))
                    nc.vector.tensor_tensor(x[k + 1][:, :], heads_out[:, 0:D], x[k][:, :], ALU.add).then_inc(S["x_done"], 1)
                else:
                    nc.vector.tensor_tensor(x[k + 1][:, :], bank[:, 2, 0:D], x[k][:, :], ALU.add).then_inc(S["x_done"], 1)

            if upto >= 2:
                dve.wait_ge(S["x_done"], 1)
                attention(0, 1, True)
            if upto >= 3:
                dve.wait_ge(S["x_done"], 2)
                layer_norm(2, x[2])
                dve.wait_ge(S["rout_in"], 48)
                dve.wait_ge(S["r_sigmoid"], 1)

                def ranks(out, vals_, num, gt, eq):
                    mine = vals_.rearrange("p (i o) -> p i o", o=1).broadcast_to((P, num, num))
                    theirs = vals_.rearrange("p (o j) -> p o j", o=1).broadcast_to((P, num, num))
                    nc.vector.tensor_tensor(gt, theirs, mine, ALU.is_gt)
                    link(nc.vector.tensor_tensor(eq, theirs, mine, ALU.is_equal))
                    link(nc.vector.tensor_tensor(eq, eq, lower[:, 0:num, 0:num], ALU.mult))
                    link(nc.vector.tensor_tensor(gt, gt, eq, ALU.add))
                    link(nc.vector.tensor_reduce(out, gt, AX.X, ALU.add))

                link(nc.vector.tensor_tensor(r_biased, r_scores, gate_b, ALU.add))
                v = r_biased.rearrange("p (g e) -> p g e", g=NG)
                nc.vector.tensor_tensor(r_pairs[:, :, 0:3], v[:, :, 0:3], v[:, :, 1:4], ALU.add)
                nc.vector.tensor_tensor(r_pairs[:, :, 3:5], v[:, :, 0:2], v[:, :, 2:4], ALU.add)
                link(nc.vector.tensor_tensor(r_pairs[:, :, 5:6], v[:, :, 0:1], v[:, :, 3:4], ALU.add))
                link(nc.vector.tensor_reduce(r_group, r_pairs, AX.X, ALU.max))
                ranks(r_grank, r_group, NG, pair_gt[:, 0:NG, 0:NG], pair_eq[:, 0:NG, 0:NG])
                link(nc.vector.tensor_scalar(r_grank, r_grank, float(TOPG), None, ALU.is_lt))
                link(nc.vector.tensor_tensor(r_masked.rearrange("p (g e) -> p g e", g=NG), v,
                                             r_grank.rearrange("p (g o) -> p g o", o=1).broadcast_to((P, NG, NE // NG)), ALU.mult))
                ranks(r_rank, r_masked, NE, pair_gt, pair_eq)
                link(nc.vector.tensor_scalar(r_sel, r_rank, float(TOPK), None, ALU.is_lt))
                link(nc.vector.tensor_tensor(r_sel, r_sel, r_scores, ALU.mult))
                link(nc.vector.tensor_reduce(r_sum[:, 0:1], r_sel, AX.X, ALU.add))
                link(nc.vector.tensor_scalar(r_sum[:, 0:1], r_sum[:, 0:1], 1e-20, None, ALU.add))
                link(nc.vector.reciprocal(r_sum[:, 1:2], r_sum[:, 0:1]))
                nc.vector.memset(combine[:, NE:NE + 2], 1.0)
                link(nc.vector.tensor_scalar(combine[:, 0:NE], r_sel, r_sum[:, 1:2], 2.5, ALU.mult, ALU.mult))
                for n in range(LOTS):
                    num = lot_num[n]
                    w = num * NI
                    h = act_h[n % 2]
                    dve.wait_ge(S["e_silu"], n + 1)
                    if n >= 2:
                        dve.wait_ge(S["e_turned"], n - 1)
                    link(nc.vector.tensor_tensor(h[:, 0:w], act_gate[n % 2][:, 0:w], bank[:, 2 * (n % 2) + 1, 0:w], ALU.mult))
                    hv = h[:, 0:w].rearrange("p (e i) -> p e i", e=num)
                    nc.vector.tensor_tensor(hv, hv, combine[:, n * EG:n * EG + num].rearrange("p (e o) -> p e o", o=1).broadcast_to((P, num, NI)),
                                            ALU.mult).then_inc(S["e_h"], 1)
                dve.wait_ge(S["e_out"], LOTS)
                nc.vector.tensor_tensor(x[3][:, :], bank[:, 6, 0:D], x[2][:, :], ALU.add).then_inc(S["x_done"], 1)
            if upto >= 4:
                dve.wait_ge(S["x_done"], 3)
                layer_norm(3, x[3])
                dve.wait_ge(S["ln_ready"], 4)
                nc.vector.tensor_scalar(xm2T[:, :, :], ln_outT[:, :, :], -2.0, None, ALU.mult).then_inc(S["xm2T_ready"], 1)
                dve.wait_ge(S["dist_sqrt"], NCTX // DCH)
                BANKS = 8
                nc.vector.memset(ones[:, :], 1.0)
                for n in range(4):
                    nc.vector.memset(pair_ring[n], BIG)
                nc.vector.memset(cost_ring, BIG)
                for n in range(3):
                    last = nc.vector.memset(bank[:, n, 0:WB], BIG)
                link(last)
                dve.sem_inc(S["shifted"], 3)
                for n in range(4):
                    dve.sem_inc(S[f"cost_stored{n}"], 16)
                nc.vector.memset(bank[0:1, 0, 0:1], 0.0).then_inc(S["scan_done"], 1)
                with dve.Fori(0, WC // 4) as i:
                    RING = 4 * WU
                    for u in range(RING):
                        n, at_u = u // WU, 1 + u * WB
                        dve.wait_ge(S["scan_done"], i * RING + (u + 1))
                        if u == 0:
                            nc.vector.tensor_copy(cost_ring[:, 0:1], cost_ring[:, RING * WB:RING * WB + 1]).then_inc(S["wrapped"], 1)
                            dve.wait_ge(S["wrapped"], i + 1)
                        if u % WU == 0:
                            dve.wait_ge(S[f"dist_in{n}"], i * 16 + 16)
                            dve.wait_ge(S[f"cost_stored{n}"], i * 16 + 16)
                        dve.wait_ge(S["shifted"], i * RING + (u + 1))
                        nc.vector.tensor_tensor_scan(cost_ring[:, at_u:at_u + WB], bank[:, u % BANKS, 0:WB],
                                                     dist_ring[n][:, (u % WU) * WB:(u % WU + 1) * WB],
                                                     cost_ring[:, at_u - 1:at_u], ALU.min, ALU.add).then_inc(S["scan_done"], 1)
                        at_p = at_u - WB if u else 1 + (RING - 1) * WB
                        nc.vector.tensor_tensor(pair_ring[u % 4][0:P - 1, :], cost_ring[0:P - 1, at_p:at_p + WB],
                                                cost_ring[0:P - 1, at_p - 1:at_p + WB - 1], ALU.min).then_inc(S["pairs_ready"], 1)
                dve.wait_ge(S["scan_done"], WT + 1)
                dve.wait_ge(S["shifted"], WT + 3)
                for n in range(4):
                    dve.wait_ge(S[f"cost_stored{n}"], 16 + 16 * (WC // 4))
                nc.vector.memset(step_one, 1.0)
                nc.vector.memset(own[:, 0:1], BIG)
                link(nc.vector.memset(left[:, 0:1], BIG))
                nc.vector.memset(left[0:1, :], BIG)
                link(nc.vector.memset(dist_c[:, BCH:BCH + 1], -1.0))
                dve.sem_inc(S["choice_done"], 1)
                for n in range(NCTX // BCH):
                    dve.wait_ge(S["own_in"], 32 * (n + 1))
                    link(nc.vector.tensor_copy(dist_c[:, 0:1], dist_c[:, BCH:BCH + 1]))
                    up_, left_, diag_ = own[:, 0:BCH], left[:, 1:BCH + 1], left[:, 0:BCH]
                    nc.vector.tensor_tensor(up_lt, up_, diag_, ALU.is_lt)
                    nc.vector.tensor_tensor(up_le, up_, left_, ALU.is_le)
                    link(nc.vector.tensor_tensor(diag, diag_, left_, ALU.is_le))
                    link(nc.vector.scalar_tensor_tensor(out=up_lt, in0=up_lt, scalar=BIG, in1=up_le, op0=ALU.mult, op1=ALU.mult))
                    link(nc.vector.scalar_tensor_tensor(out=diag, in0=diag, scalar=0.5, in1=up_lt, op0=ALU.mult, op1=ALU.add))
                    link(nc.vector.tensor_tensor_scan(dist_c[:, 1:BCH + 1], step_one, diag, dist_c[:, 0:1], ALU.add, ALU.min))
                    if n >= 1:
                        dve.wait_ge(S["deltas_stored"], 16 * n)
                    nc.vector.scalar_tensor_tensor(out=deltas, in0=dist_c[:, 0:BCH], scalar=1.0, in1=dist_c[:, 1:BCH + 1],
                                                   op0=ALU.add, op1=ALU.subtract).then_inc(S["choice_done"], 1)
                link(nc.vector.memset(bounds[:, P:P + 1], float(NCTX - 1)))
                dve.wait_ge(S["deltas_x_in"], 16)
                for j in range(P - 1, -1, -1):
                    if j < P - 1:
                        dve.wait_ge(S["bound_ready"], P - 1 - j)
                    at_j = bounds[:, P:P + 1] if j == P - 1 else bank[:, (j + 1) % 2, j + 1:j + 2]
                    nc.vector.scalar_tensor_tensor(out=picked, in0=rows_i[:, :], scalar=at_j, in1=deltas_x[:, j, :],
                                                   op0=ALU.is_le, op1=ALU.mult, accum_out=picked_sum[:, j:j + 1]).then_inc(S["picked_ready"], 1)
                dve.wait_ge(S["bound_ready"], P)
                for r in range(2):
                    last = nc.vector.tensor_copy(bounds[:, r:P:2], bank[:, r, r:P:2])
                link(last)
                for m in range(FR // MF):
                    if m >= 1:
                        dve.wait_ge(S["masks_used"], m)
                    ri = rows_i[:, m * MF:(m + 1) * MF].rearrange("p (f o) -> p f o", o=1).broadcast_to((P, MF, P))
                    lo = bounds[:, 0:P].rearrange("p (o j) -> p o j", o=1).broadcast_to((P, MF, P))
                    hi = bounds[:, 1:P + 1].rearrange("p (o j) -> p o j", o=1).broadcast_to((P, MF, P))
                    link(nc.vector.tensor_tensor(masks[0], ri, lo, ALU.is_ge))
                    mask_hi = deltas_x[:, 0:MF * P // FR + 1, :].rearrange("p a b -> p (a b)")[:, 0:MF * P].rearrange("p (f j) -> p f j", f=MF)
                    link(nc.vector.tensor_tensor(mask_hi, ri, hi, ALU.is_le))
                    nc.vector.tensor_tensor(masks[0], masks[0], mask_hi, ALU.mult).then_inc(S["masks_ready"], 1)
                dve.wait_ge(S["masks_used"], FR // MF)
                nc.vector.tensor_tensor(x[4][:, :], bank[:, 4, 0:D], x[3][:, :], ALU.add).then_inc(S["x_done"], 1)
            if upto >= 5:
                dve.wait_ge(S["x_done"], 4)
                attention(1, 4, False)
            if upto >= 6:
                dve.wait_ge(S["x_done"], 5)
                layer_norm(5, x[5])
                dve.wait_ge(S["f_logits"], 1)
                dve.wait_ge(S["f_in"], 16 * 7)
                link(nc.vector.tensor_copy(f_logit, bank[:, 4, 0:FE]))
                link(nc.vector.tensor_reduce(f_max[:, 0:1], f_logit, AX.X, ALU.max))
                link(nc.vector.scalar_tensor_tensor(out=f_val, in0=f_logit, scalar=f_max[:, 0:1], in1=f_ramp, op0=ALU.is_ge, op1=ALU.mult))
                link(nc.vector.tensor_reduce(f_max[:, 1:2], f_val, AX.X, ALU.max))
                link(nc.vector.tensor_scalar(f_mask, f_ramp, f_max[:, 1:2], None, ALU.is_equal))
                nc.vector.memset(f_hT[0][FH:FH + 1, :], 1.0)
                link(nc.vector.memset(f_hT[1][FH:FH + 1, :], 1.0))
                layer_norm(6, ln_out)
                dve.wait_ge(S["ln_ready"], 7)
                nc.vector.tensor_copy(x[6][:, :], x[5][:, :]).then_inc(S["f_added"], 1)

                def add(e):
                    dve.wait_ge(S["f_out"], e + 1)
                    dve.wait_ge(S["f_added"], e + 1)
                    ins = nc.vector.scalar_tensor_tensor(out=x[6][:, :], in0=bank[:, 2 + e % 2, 0:D], scalar=f_mask[:, e:e + 1],
                                                         in1=x[6][:, :], op0=ALU.mult, op1=ALU.add)
                    ins.then_inc(S["x_done"] if e == FE - 1 else S["f_added"], 1)

                for e in range(FE):
                    if e >= 2:
                        dve.wait_ge(S["f_h"], e - 1)
                    for c in range(DC):
                        last = nc.vector.tensor_scalar(f_xT[e % 2][:, c, :], ln_outT[:, c, :], f_s[:, c, e:e + 1], f_b[:, c, e:e + 1], ALU.mult, ALU.add)
                    last.then_inc(S["f_xT_ready"], 1)
                    if e >= 1:
                        add(e - 1)
                add(FE - 1)

        @block.tensor
        def _(pe):
            def turn_ln(k):
                pe.wait_ge(S["ln_rows"], k + 1)
                for c in range(DC):
                    last = nc.tensor.transpose(bank[:, 7, c * P:(c + 1) * P], ln_out[:, c * P:(c + 1) * P], ident[:, :])
                last.then_inc(S["ln_turned"], 1)

            pe.wait_ge(S["xw_in"], 16 * 8)
            pe.wait_ge(S["const_in"], 64)
            pe.wait_ge(S["q_taken"], 1)

            def norm_sums(i, n, m):
                for c in range(DC):
                    last = nc.tensor.matmul(bank[0:1, 7, 0:448], ones_col[:, 0:1], squares[:, c, m * 448:(m + 1) * 448],
                                            start=(c == 0), stop=(c == DC - 1))
                last.then_inc(S["vproj_ready"], 1)
                return last

            with pe.Fori(0, NLCH // 2) as i:
                for n in range(2):
                    pe.wait_ge(S[f"ctxT_in{n}"], i * 16 + 16)
                    for m, g, lo in ((0, 0, 0), (1, 0, 448), (2, 1, 0), (3, 2, 0), (3, 3, 0)):
                        num = min(448, LCH >> g)
                        col = 224 if g == 3 else 0
                        if g < 3:
                            pe.wait_ge(S["kproj_taken"], i * 8 + (4 * n + m + 1))
                        for c in range(DC):
                            last = nc.tensor.matmul(bank[:, m, col:col + num], w_k[:, c, g * P:(g + 1) * P],
                                                    ctxT[n][:, c, lo:lo + (num - 1) * (1 << g) + 1:1 << g],
                                                    start=(c == 0), stop=(c == DC - 1))
                        if g != 2:
                            last.then_inc(S["kproj_ready"], 1)
                    pe.wait_ge(S["squares_ready"], i * 2 + n + 1)
                    pe.wait_ge(S["vproj_taken"], i * 10 + (5 * n + 5))
                    norm_sums(i, n, 0)
                    for m, classes in enumerate(VBANKS):
                        pe.wait_ge(S["vproj_taken"], i * 10 + (5 * n + 2 + m))
                        for r in classes:
                            col, num = (SLOT[r] - SLOT[classes[0]]) * VW, SERVES[r] * VW
                            for c in range(DC):
                                last = nc.tensor.matmul(bank[0:KT, 4 + m, col:col + num], ctxT[n][:, c, r:r + 8 * (KT - 1) + 1:8],
                                                        w_v[:, c, 0:num], start=(c == 0), stop=(c == DC - 1))
                        last.then_inc(S["vproj_ready"], 1)
                    pe.wait_ge(S["vproj_taken"], i * 10 + (5 * n + 6))
                    norm_sums(i, n, 1)
            turn_ln(0)
            pe.wait_ge(S["ln_ready"], 1)
            pe.wait_ge(S["kproj_taken"], 4 * NLCH + 4)
            for g in range(XG):
                for c in range(DC):
                    last = nc.tensor.matmul(bank[:, 0, g * P:(g + 1) * P], w_q[:, c, g * P:(g + 1) * P], ln_outT[:, c, :],
                                            start=(c == 0), stop=(c == DC - 1))
            last.then_inc(S["q_ready"], 1)
            pe.wait_ge(S["q_blocks"], 1)
            pe.wait_ge(S["vproj_taken"], 5 * NLCH + 5)
            n = 0
            for g in range(XG):
                for k in range(KEYS[g] // MCH):
                    s = n % 2
                    if n >= 2:
                        pe.wait_ge(S["max_taken"], n - 1)
                    for h in range(XH):
                        last = nc.tensor.matmul(bank[:, 4 * s + h, 0:MCH], query_blocks[:, g, h * P:(h + 1) * P],
                                                keysT[g][:, k * MCH:(k + 1) * MCH], start=True, stop=True)
                    last.then_inc(S["max_scores"], 1)
                    n += 1
            pe.wait_ge(S["negmax_ready"], 1)
            for g in range(XG):
                last = nc.tensor.transpose(bank[:, 0, g * P:(g + 1) * P], neg_max[:, g * P:(g + 1) * P], ident[:, :])
            last.then_inc(S["negmax_turned"], 1)
            pe.wait_ge(S["qmax_ready"], 1)

            def attend(u):
                pe.wait_ge(S["probs_ready"], u + 1)
                for j, (g, c, r) in enumerate(UNITS[u]):
                    slot = (SLOT[r] + g) * VW
                    if (c, r) == (0, 0) and g >= 2:
                        pe.wait_ge(S["att_copied"], g - 1)
                    end = (c, r) == (NLCH - 1, 8 - (1 << g))
                    last = nc.tensor.matmul(bank[0:VW, 6 + g % 2, :], vals[:, c, slot:slot + VW], probs[u % 3][:, j, :],
                                            start=(c, r) == (0, 0), stop=end)
                last.then_inc(S["probs_used"], 1)

            for u, unit in enumerate(UNITS):
                s = u % 3
                if u >= 3:
                    pe.wait_ge(S["probs_ready"], u - 2)
                for j, (g, c, r) in enumerate(unit):
                    first, step = (c * LCH + r) >> g, 8 >> g
                    last = nc.tensor.matmul(bank[0:KT, 2 * s + j, :], keysT[g][:, first:first + step * (KT - 1) + 1:step],
                                            query_blocks[:, g, :], start=True, stop=True)
                last.then_inc(S["scores_ready"], 1)
                if u >= 2:
                    attend(u - 2)
            attend(len(UNITS) - 2)
            attend(len(UNITS) - 1)
            pe.wait_ge(S["probs_ready"], len(UNITS))
            for g in range(XG):
                pe.wait_ge(S["att_copied"], g + 1)
                for h in range(XH):
                    last = nc.tensor.transpose(bank[:, g, h * VW:(h + 1) * VW], att_sums[g % 2][:, h * P:(h + 1) * P], ident[0:VW, 0:VW])
                last.then_inc(S["att_turned"], 1)
            pe.wait_ge(S["xo_ready"], 1)
            for c in range(DC):
                last = nc.tensor.transpose(bank[:, 5, c * P:(c + 1) * P], xo[:, c * P:(c + 1) * P], ident[:, :])
            last.then_inc(S["xo_turned"], 1)
            pe.wait_ge(S["xoT_ready"], 1)
            for c in range(DC):
                last = nc.tensor.matmul(bank[:, 4, 0:D], xoT[:, c, :], w_o[:, c, :], start=(c == 0), stop=(c == DC - 1))
            last.then_inc(S["x_proj"], 1)


            def attention(z, k):
                turn_ln(k)
                pe.wait_ge(S["ln_ready"], k + 1)
                pe.wait_ge(S["x_done"], k)
                pe.wait_ge(S[f"wa_in{z}"], 16 * (10 if z == 0 else 5))
                if z == 1:
                    for c in range(DC):
                        last = nc.tensor.matmul(bank[0:AD, 6, 0:P], lat_down[:, c, :], ln_outT[:, c, :], start=(c == 0), stop=(c == DC - 1))
                    last.then_inc(S["lat_turned"], 1)
                for n in range(3):
                    if z == 1 and n == 1:
                        pe.wait_ge(S["latT_ready"], 1)
                    for half in range(2):
                        cols = slice(512 * half, 512 * (half + 1))
                        if z == 0 or n == 0:
                            w = ((wa_q, wa_k, wa_v) if z == 0 else (lat_q,))[n]
                            for c in range(DC):
                                last = nc.tensor.matmul(bank[:, 2 * n + half, :], ln_outT[:, c, :], w[:, c, cols], start=(c == 0), stop=(c == DC - 1))
                        else:
                            up = (lat_up, lat_up_v)[n - 1]
                            last = nc.tensor.matmul(bank[:, 2 * n + half, :], latT[0:AD, :], up[0:AD, half, :], start=True, stop=True)
                    last.then_inc(S[f"a_proj{z}"], 1)
                for n in range(2):
                    pe.wait_ge(S[f"a_rows{z}"], n + 1)
                    for b in range(AB):
                        last = nc.tensor.transpose(bank[:, 2 * n + b // 4, (b % 4) * P:(b % 4 + 1) * P], proj[n][:, b * P:(b + 1) * P], ident[:, :])
                    last.then_inc(S[f"a_turned{z}"], 1)
                pe.wait_ge(S[f"a_qkT{z}"], 2)
                pe.wait_ge(S[f"a_rows{z}"], 3)
                for n in range(4):
                    r = n // 2
                    for j in range(4):
                        b = (n % 2) * 4 + j
                        last = nc.tensor.matmul(bank[:, 4 + n, j * P:(j + 1) * P], qkT[0][AD * r:AD * r + AD, b, :], qkT[1][AD * r:AD * r + AD, b, :],
                                                start=True, stop=True)
                    last.then_inc(S[f"a_scores{z}"], 1)
                for n in range(4):
                    pe.wait_ge(S[f"a_probs{z}"], n + 1)
                    for j in range(4):
                        last = nc.tensor.transpose(bank[:, n, j * P:(j + 1) * P], scores_sb[:, 4 * n + j, :], ident[:, :])
                    last.then_inc(S[f"a_probs_turned{z}"], 1)
                for n in range(4):
                    pe.wait_ge(S[f"a_probsT{z}"], n + 1)
                    for j in range(4):
                        h = 2 * ((n % 2) * 4 + j) + n // 2
                        last = nc.tensor.matmul(bank[:, 4 + h // 8, (h % 8) * AD:(h % 8 + 1) * AD], probsT[:, 4 * n + j, :], proj[2][:, h * AD:(h + 1) * AD],
                                                start=True, stop=True)
                    last.then_inc(S[f"a_values{z}"], 1)
                pe.wait_ge(S[f"a_heads{z}"], 1)
                for b in range(AB):
                    last = nc.tensor.transpose(bank[:, b // 4, (b % 4) * P:(b % 4 + 1) * P], heads_out[:, b * P:(b + 1) * P], ident[:, :])
                last.then_inc(S[f"a_heads_turned{z}"], 1)
                pe.wait_ge(S[f"a_headsT{z}"], 1)
                w = wa_o if z == 0 else lat_o
                for b in range(AB):
                    last = nc.tensor.matmul(bank[:, 2, 0:D], heads_outT[:, b, :], w[:, b, :], start=(b == 0), stop=(b == AB - 1))
                last.then_inc(S[f"a_out{z}"], 1)

            if upto >= 2:
                attention(0, 1)
            if upto >= 3:
                turn_ln(2)
                pe.wait_ge(S["ln_ready"], 3)
                pe.wait_ge(S["rout_in"], 48)
                for c in range(DC):
                    last = nc.tensor.matmul(bank[:, 4, 0:NE], ln_outT[:, c, :], gate_w[:, c, :], start=(c == 0), stop=(c == DC - 1))
                last.then_inc(S["r_logits"], 1)

                def up(n):
                    w = lot_num[n] * NI
                    pe.wait_ge(*((S["lots_in0"], 16 * 15) if n < 5 else (S["lots_in1"], 16 * 12)))
                    if n >= 2:
                        pe.wait_ge(S["e_h"], n - 1)
                    for m, t in enumerate((lot_gate, lot_up)):
                        for c in range(DC):
                            last = nc.tensor.matmul(bank[:, 2 * (n % 2) + m, 0:w], ln_outT[:, c, :], t[n][:, c, :], start=(c == 0), stop=(c == DC - 1))
                    last.then_inc(S["e_up"], 1)

                def turn(n):
                    pe.wait_ge(S["e_h"], n + 1)
                    if n >= 2:
                        pe.wait_ge(S["e_hT"], n - 1)
                    if n == 0:
                        pe.wait_ge(S["r_sigmoid"], 1)
                    for e in range(lot_num[n]):
                        last = nc.tensor.transpose(bank[:, 4 + n % 2, e * P:(e + 1) * P], act_h[n % 2][:, e * NI:(e + 1) * NI], ident[:, :])
                    last.then_inc(S["e_turned"], 1)

                def down(n):
                    pe.wait_ge(S["e_hT"], n + 1)
                    for e in range(lot_num[n]):
                        last = nc.tensor.matmul(bank[:, 6, 0:D], act_hT[n % 2][:, e, :], lot_down[n][:, e, :],
                                                start=(n + e == 0), stop=(n == LOTS - 1 and e == lot_num[n] - 1))
                    last.then_inc(S["e_out"], 1)

                up(0)
                for n in range(LOTS):
                    if n + 1 < LOTS:
                        up(n + 1)
                    turn(n)
                    if n >= 1:
                        down(n - 1)
                down(LOTS - 1)
            if upto >= 4:
                turn_ln(3)
                pe.wait_ge(S["xm2T_ready"], 1)
                for n in range(NCTX // DCH):
                    s = n % 4
                    pe.wait_ge(S[f"dchunk_in{s}"], 32 * (n // 4 + 1))
                    if n >= 4:
                        pe.wait_ge(S["dist_relu"], n - 3)
                    for c in range(DC):
                        nc.tensor.matmul(bank[:, s, 0:DCH], xm2T[:, c, :], ctxT_ring[s][:, c, :], start=(c == 0), stop=False)
                    nc.tensor.matmul(bank[:, s, 0:DCH], ones_row[0:1, :], norm_ring[s], start=False, stop=True).then_inc(S["dist_sum"], 1)
                with pe.Fori(0, WC // 4) as i:
                    RING = 4 * WU
                    for u in range(RING):
                        pe.wait_ge(S["pairs_ready"], i * RING + (u + 1))
                        nc.tensor.matmul(bank[:, (u + 3) % 8, 0:WB], shift[:, :], pair_ring[u % 4], start=True, stop=True).then_inc(S["shifted"], 1)
                for j in range(P - 1, -1, -1):
                    pe.wait_ge(S["picked_ready"], P - j)
                    nc.tensor.matmul(bank[:, j % 2, j:j + 1], ones[:, :], picked_sum[:, j:j + 1], start=True, stop=True).then_inc(S["bound_ready"], 1)
                pe.wait_ge(S["ctx_in"], 16)
                for m in range(FR // MF):
                    pe.wait_ge(S["masks_ready"], m + 1)
                    for f in range(MF):
                        n = m * MF + f
                        last = nc.tensor.matmul(bank[:, 4, 0:D], masks[0][:, f, :], ctx_rows[:, n, :], start=(n == 0), stop=(n == FR - 1))
                    last.then_inc(S["masks_used"], 1)
            if upto >= 5:
                attention(1, 4)
            if upto >= 6:
                turn_ln(5)
                pe.wait_ge(S["ln_ready"], 6)
                pe.wait_ge(S["f_in"], 16 * 7)
                for c in range(DC):
                    last = nc.tensor.matmul(bank[:, 4, 0:FE], ln_outT[:, c, :], f_g[:, c, :], start=(c == 0), stop=(c == DC - 1))
                last.then_inc(S["f_logits"], 1)
                turn_ln(6)

                def out(e):
                    pe.wait_ge(S["f_hT_ready"], e + 1)
                    if e >= 2:
                        pe.wait_ge(S["f_added"], e)
                    nc.tensor.matmul(bank[:, 2 + e % 2, 0:D], f_hT[e % 2], f_w2[:, e, :], start=True, stop=True).then_inc(S["f_out"], 1)

                for e in range(FE):
                    pe.wait_ge(S["f_xT_ready"], e + 1)
                    if e >= 2:
                        pe.wait_ge(S["f_hT_ready"], e - 1)
                    for c in range(DC):
                        last = nc.tensor.matmul(bank[0:FH, e % 2, 0:P], f_w1[:, c, e * FH:(e + 1) * FH], f_xT[e % 2][:, c, :],
                                                start=(c == 0), stop=(c == DC - 1))
                    last.then_inc(S["f_h"], 1)
                    if e >= 1:
                        out(e - 1)
                out(FE - 1)


def host_arrays(inputs):
    f = {n: np.asarray(v) for n, v in inputs.items()}
    out = {}
    ctx = f["ctx_1024"][0]
    out["x"] = np.ascontiguousarray(f["x"][0])
    out["ctx"] = np.ascontiguousarray(ctx)
    out["ctxT"] = np.ascontiguousarray(ctx.T)
    out["ident"] = np.eye(P, dtype=np.float32)
    wk = np.zeros((D, XG, XH, 32), np.float32)
    wq = np.zeros((D, XG, XH, 32), np.float32)
    wv = np.zeros((D, XG, XH, XD + 1), np.float32)
    bk = np.zeros((XH, 32, XG), np.float32)
    bq = np.zeros((XH, 32, XG), np.float32)
    bv = np.zeros((XG, XH, XD + 1), np.float32)
    wk[..., 0:XD] = f["L0_xattn_Wk"].T.reshape(D, XH, XG, XD).transpose(0, 2, 1, 3)
    wq[..., 0:XD] = f["L0_xattn_Wq"].T.reshape(D, XH, XG, XD).transpose(0, 2, 1, 3)
    wv[..., 0:XD] = f["L0_xattn_Wv"].T.reshape(D, XH, XG, XD).transpose(0, 2, 1, 3)
    bk[:, 0:XD] = f["L0_xattn_bk"].reshape(XH, XG, XD).transpose(0, 2, 1)
    bq[:, 0:XD] = f["L0_xattn_bq"].reshape(XH, XG, XD).transpose(0, 2, 1)
    bv[:, :, 0:XD] = f["L0_xattn_bv"].reshape(XH, XG, XD).transpose(1, 0, 2)
    bk[:, XD] = 1.0
    bv[..., XD] = 1.0
    out["xw_k"], out["xw_q"], out["xw_v"] = wk.reshape(D, -1), wq.reshape(D, -1), wv.reshape(D, -1)
    out["xb_k"], out["xb_q"], out["xb_v"] = bk.reshape(P, XG), bq.reshape(P, XG), np.concatenate([bv[0:SERVES[r]].ravel() for r in CLASSES]).reshape(1, -1)
    out["xw_o"] = np.ascontiguousarray(f["L0_xattn_Wo"].T)
    out["xb_o"] = f["L0_xattn_bo"].reshape(1, D)
    for n in "qkv":
        out["aw_" + n] = np.ascontiguousarray(f["L0_attn_w" + n].T)
        out["ab_" + n] = f["L0_attn_b" + n].reshape(1, AW)
    out["aw_o"] = np.ascontiguousarray(f["L0_attn_wo"].T)
    out["ab_o"] = f["L0_attn_bo"].reshape(1, D)
    theta = np.float32(10000.0) ** (np.arange(0, AD, 2, dtype=np.float32) / np.float32(AD))
    freqs = np.arange(P, dtype=np.float32)[:, None] * (np.float32(1.0) / theta)[None, :]
    emb = np.concatenate([freqs, freqs], axis=-1).astype(np.float32)
    out["rope_cos"] = np.cos(emb).astype(np.float32)
    out["rope_sin"] = (np.sin(emb) * np.where(np.arange(AD) % 2, 1.0, -1.0)).astype(np.float32)
    out["causal"] = np.where(np.triu(np.ones((P, P), bool), 1), -BIG, 0.0).astype(np.float32)
    out["rw"] = np.ascontiguousarray(f["L0_ffn_gate_w"].T)
    out["rb"] = f["L0_ffn_gate_bias"].reshape(1, NE)
    out["lower"] = np.tril(np.ones((NE, NE), np.float32), -1).reshape(1, -1)
    for n in ("gate", "up"):
        out["ew_" + n] = np.ascontiguousarray(f["L0_ffn_w_" + n].reshape(NE * NI, D).T)
        out["esh_" + n] = np.ascontiguousarray(f["L0_ffn_sh_" + n].T)
    out["ew_down"] = np.ascontiguousarray(f["L0_ffn_w_down"].transpose(2, 0, 1))
    out["esh_down"] = np.ascontiguousarray(f["L0_ffn_sh_down"].T)
    out["shift"] = np.roll(np.eye(P, dtype=np.float32), 1, axis=1)
    out["rows_i"] = np.arange(NCTX, dtype=np.float32).reshape(P, FR)
    out["lw_q"] = f["L1_attn_Wq"].reshape(D, AW)
    out["lw_down"] = f["L1_attn_Wkv_down"]
    out["lw_k"] = f["L1_attn_Wk_up"].reshape(AD, AW)
    out["lw_v"] = f["L1_attn_Wv_up"].reshape(AD, AW)
    out["lw_o"] = f["L1_attn_Wout"].reshape(AW, D)
    out["fw1"] = np.ascontiguousarray(f["L1_ffn_W1"].transpose(1, 0, 2).reshape(D, FE * FH))
    out["fw2"] = np.ascontiguousarray(np.concatenate([f["L1_ffn_W2"], f["L1_ffn_b2"][:, None, :]], axis=1).transpose(1, 0, 2))
    out["fg"] = np.ascontiguousarray(f["L1_ffn_Wg"].T)
    out["fs"] = np.ascontiguousarray(f["L1_ffn_ln_scale"].T)
    out["fb"] = np.ascontiguousarray(f["L1_ffn_ln_bias"].T)
    out["fb1"] = np.ascontiguousarray(f["L1_ffn_b1"].T)
    out["ramp"] = np.arange(FE, 0, -1, dtype=np.float32).reshape(1, FE)
    return out


def kernel(**inputs):
    import concourse.bacc as bacc
    from concourse.bass_utils import run_bass_kernel_spmd

    arrays = host_arrays(inputs)
    nc = bacc.Bacc("TRN2", target_bir_lowering=False, num_devices=1)
    a = {n: nc.dram_tensor(f"in_{n}", v.shape, mybir.dt.from_np(v.dtype), kind="ExternalInput").ap() for n, v in arrays.items()}
    a["out"] = nc.dram_tensor("out_x", [P, D], F32, kind="ExternalOutput").ap()
    build_program(nc, a)
    r = run_bass_kernel_spmd(nc, [{f"in_{n}": v for n, v in arrays.items()}], core_ids=[0])
    return np.asarray(r.results[0]["out_x"]).reshape(1, P, D)
```
